# Optimizing a Trainium2 kernel written in Bass

```python
import numpy as np
import jax
import jax.numpy as jnp

def _softmax(x, axis=-1):
    return jax.nn.softmax(x, axis=axis)

def _gelu(x):
    return jax.nn.gelu(x, approximate=True)

def _silu(x):
    return jax.nn.silu(x)

def _sigmoid(x):
    return jax.nn.sigmoid(x)

def _layernorm(x, axis=-1, eps=1e-05):
    m = jnp.mean(x, axis=axis, keepdims=True)
    v = jnp.var(x, axis=axis, keepdims=True)
    return (x - m) / jnp.sqrt(v + eps)

def _scatter_add(tgt, idx, src, axis=0):
    return tgt.at[idx].add(src)

def _segment_sum(src, seg, n):
    return jax.ops.segment_sum(src, seg, n)
kernel_name = 'mk_sandwich_d1_jaxref_r4_d6cbc8'

def setup_inputs(seed: int=0):
    np.random.seed(seed)
    _w = jnp.asarray

    def _L0_attn_setup():
        import jax, jax.numpy as jnp
        import numpy as np
        B, T, D, N, R = (2, 512, 256, 16, 64)
        key = jax.random.key(seed)
        ks = jax.random.split(key, 8)
        sc = 0.02
        return {'x': jax.random.normal(ks[0], (B, T, D), jnp.float32), 'W_in': jax.random.normal(ks[1], (2 * D, D), jnp.float32) * sc, 'conv_w': jax.random.normal(ks[2], (D, 3), jnp.float32) * sc, 'W_x': jax.random.normal(ks[3], (R + 2 * N, D), jnp.float32) * sc, 'W_dt': jax.random.normal(ks[4], (D, R), jnp.float32) * sc, 'b_dt': jnp.ones((D,), jnp.float32), 'A_log': jnp.full((D, N), -2.0, jnp.float32), 'D_param': jnp.ones((D,), jnp.float32), 'W_C': jax.random.normal(ks[5], (D, N), jnp.float32) * sc, 'W_out': jax.random.normal(ks[6], (D, D), jnp.float32) * sc}
    _L0_attn_in = _L0_attn_setup()

    def _L0_ffn_setup():
        import jax, jax.numpy as jnp
        import numpy as np
        TOP_K = 2
        key = jax.random.key(seed)
        ks = jax.random.split(key, 6)
        B, S, H, F, E = (4, 512, 256, 1024, 8)
        x = jax.random.normal(ks[0], (B, S, H), dtype=jnp.float32)
        gate_w = jax.random.normal(ks[1], (E, H), dtype=jnp.float32) * 0.02
        W1 = jax.random.normal(ks[2], (E, H, F), dtype=jnp.float32) * (1.0 / np.sqrt(H))
        b1 = jnp.zeros((E, F), dtype=jnp.float32)
        W2 = jax.random.normal(ks[3], (E, F, H), dtype=jnp.float32) * (1.0 / np.sqrt(F))
        b2 = jnp.zeros((E, H), dtype=jnp.float32)
        sW1 = jax.random.normal(ks[4], (H, F), dtype=jnp.float32) * (1.0 / np.sqrt(H))
        sb1 = jnp.zeros((F,), dtype=jnp.float32)
        sW2 = jax.random.normal(ks[5], (F, H), dtype=jnp.float32) * (1.0 / np.sqrt(F))
        sb2 = jnp.zeros((H,), dtype=jnp.float32)
        return {'x': x, 'gate_w': gate_w, 'W1': W1, 'b1': b1, 'W2': W2, 'b2': b2, 'sW1': sW1, 'sb1': sb1, 'sW2': sW2, 'sb2': sb2}
    _L0_ffn_in = _L0_ffn_setup()
    _d = {'L0_attn_x': _L0_attn_in['x'], 'L0_attn_W_in': _L0_attn_in['W_in'], 'L0_attn_conv_w': _L0_attn_in['conv_w'], 'L0_attn_W_x': _L0_attn_in['W_x'], 'L0_attn_W_dt': _L0_attn_in['W_dt'], 'L0_attn_b_dt': _L0_attn_in['b_dt'], 'L0_attn_A_log': _L0_attn_in['A_log'], 'L0_attn_D_param': _L0_attn_in['D_param'], 'L0_attn_W_C': _L0_attn_in['W_C'], 'L0_attn_W_out': _L0_attn_in['W_out'], 'L0_ffn_gate_w': _L0_ffn_in['gate_w'], 'L0_ffn_W1': _L0_ffn_in['W1'], 'L0_ffn_b1': _L0_ffn_in['b1'], 'L0_ffn_W2': _L0_ffn_in['W2'], 'L0_ffn_b2': _L0_ffn_in['b2'], 'L0_ffn_sW1': _L0_ffn_in['sW1'], 'L0_ffn_sb1': _L0_ffn_in['sb1'], 'L0_ffn_sW2': _L0_ffn_in['sW2'], 'L0_ffn_sb2': _L0_ffn_in['sb2']}
    _x0 = _d['L0_attn_x']
    _d['L0_attn_x'] = jax.random.normal(jax.random.fold_in(jax.random.key(seed), 1), (4, 1024, 256), dtype=_x0.dtype)
    del _x0
    return _d

def reference(L0_attn_x, L0_attn_W_in, L0_attn_conv_w, L0_attn_W_x, L0_attn_W_dt, L0_attn_b_dt, L0_attn_A_log, L0_attn_D_param, L0_attn_W_C, L0_attn_W_out, L0_ffn_gate_w, L0_ffn_W1, L0_ffn_b1, L0_ffn_W2, L0_ffn_b2, L0_ffn_sW1, L0_ffn_sb1, L0_ffn_sW2, L0_ffn_sb2):

    def _L0_attn_ref(x, W_in, conv_w, W_x, W_dt, b_dt, A_log, D_param, W_C, W_out):
        import jax, jax.numpy as jnp
        import numpy as np
        B, T, D, N, R = (2, 512, 256, 16, 64)
        xz = jnp.einsum('btd,ed->bte', x, W_in)
        xc, z = jnp.split(xz, 2, axis=-1)
        xp = jnp.pad(xc, ((0, 0), (1, 1), (0, 0)))
        xconv = xp[:, :-2] * conv_w[:, 0] + xp[:, 1:-1] * conv_w[:, 1] + xp[:, 2:] * conv_w[:, 2]
        xs = jax.nn.silu(xconv)
        x_dbl = jnp.einsum('btd,ed->bte', xs, W_x)
        dt_param = x_dbl[..., :R]
        Bp = x_dbl[..., R:R + N]
        Cp = x_dbl[..., R + N:]
        dt = jax.nn.softplus(dt_param @ W_dt.T + b_dt) + 1e-05
        A_disc = jnp.exp(-jnp.exp(A_log)[None, None] * dt[..., None])
        Bx = Bp[:, :, None, :] * dt[..., None] * xs[..., None]
        C = Cp @ W_C.T

        def step(s, inp):
            A_t, Bx_t = inp
            s = A_t * s + Bx_t
            return (s, s.sum(-1))
        s0 = jnp.zeros((x.shape[0], D, N), x.dtype)
        _, ssum = jax.lax.scan(step, s0, (A_disc.transpose(1, 0, 2, 3), Bx.transpose(1, 0, 2, 3)))
        ssum = ssum.transpose(1, 0, 2)
        y = C * ssum + D_param * xs
        return jnp.einsum('btd,ed->bte', y, W_out) * jax.nn.silu(z)

    def _L0_ffn_ref(x, gate_w, W1, b1, W2, b2, sW1, sb1, sW2, sb2):
        import jax, jax.numpy as jnp
        import numpy as np
        TOP_K = 2
        B, S, H = x.shape
        E = gate_w.shape[0]
        x_flat = x.reshape(-1, H)
        logits = x_flat @ gate_w.T
        probs = jax.nn.softmax(logits.astype(jnp.float32), axis=-1)
        top_w, sel = jax.lax.top_k(probs, TOP_K)
        top_w = top_w / jnp.sum(top_w, axis=-1, keepdims=True)
        combine = jnp.sum(jax.nn.one_hot(sel, E, dtype=top_w.dtype) * top_w[..., None], axis=1)
        combine = combine.astype(x.dtype)
        h = jax.nn.gelu(jnp.einsum('th,ehf->tef', x_flat, W1) + b1[None], approximate=False)
        y = jnp.einsum('tef,efh->teh', h, W2) + b2[None]
        out = jnp.einsum('teh,te->th', y, combine)
        sh = jax.nn.gelu(x_flat @ sW1 + sb1, approximate=False)
        out = out + sh @ sW2 + sb2
        return out.reshape(B, S, H)
    x = L0_attn_x
    x = x + _layernorm(_L0_attn_ref(_layernorm(x, axis=-1), L0_attn_W_in, L0_attn_conv_w, L0_attn_W_x, L0_attn_W_dt, L0_attn_b_dt, L0_attn_A_log, L0_attn_D_param, L0_attn_W_C, L0_attn_W_out), axis=-1)
    x = x + _layernorm(_L0_ffn_ref(_layernorm(x, axis=-1), L0_ffn_gate_w, L0_ffn_W1, L0_ffn_b1, L0_ffn_W2, L0_ffn_b2, L0_ffn_sW1, L0_ffn_sb1, L0_ffn_sW2, L0_ffn_sb2), axis=-1)
    return x

_drawn_inputs = setup_inputs


def setup_inputs(seed=0):
    import zlib

    import numpy as np

    out = dict(_drawn_inputs(seed))
    spreads = {'L0_attn_b_dt': (1.0, 0.6),
     'L0_attn_A_log': (-2.0, 0.6),
     'L0_attn_D_param': (1.0, 0.2),
     'L0_ffn_b1': (0.0, 0.1),
     'L0_ffn_b2': (0.0, 0.1),
     'L0_ffn_sb1': (0.0, 0.1),
     'L0_ffn_sb2': (0.0, 0.1)}
    factors = {'L0_attn_W_x': 50.436, 'L0_attn_W_dt': 64.0, 'L0_attn_W_C': 47.309}
    for name, (base, spread) in spreads.items():
        noise = np.random.default_rng([zlib.crc32(name.encode()), seed]).standard_normal(out[name].shape)
        drawn = base * np.exp(spread * noise) if base else spread * noise
        out[name] = jnp.asarray(drawn.astype(out[name].dtype))
    for name, factor in factors.items():
        out[name] = (out[name] * factor).astype(out[name].dtype)
    return out
```

```python
import concourse.bass as bass
from concourse import mybir
from contextlib import ExitStack

T, D, F, E, NB, TB = 4096, 256, 1024, 8, 4, 1024
NTOK = T // 128
ROWS = 256
NTILE = (2 * T + E * (ROWS - 1)) // ROWS
NCOL = NTILE * ROWS // 128
CI, CT, CO, CM8, CTH, CTI, CMH, CEP = 0, 128, 256, 384, 392, 408, 448, 456
CW = 457


class Queues:

    ENGINES = ("tensor", "vector", "scalar", "gpsimd", "sync")

    def __init__(self, sem):
        self.items = {e: [] for e in self.ENGINES}
        self.sems = {e: sem("s_" + e) for e in self.ENGINES}
        self.count = {e: 0 for e in self.ENGINES}

    def op(self, engine, fn, *after):
        self.count[engine] += 1
        self.items[engine].append((fn, after, self.sems[engine], 1))
        return (self.sems[engine], self.count[engine], engine)

    def dma(self, engine, lane, fn, *after):
        lane.count += 16
        self.items[engine].append((fn, after, lane.sem, 16))
        return (lane.sem, lane.count, lane.sem)

    def play(self, engine, eng):
        seen = {}
        for fn, after, sem, n in self.items[engine]:
            for s, value, key in after:
                if seen.get(key, 0) < value:
                    eng.wait_ge(s, value)
                    seen[key] = value
            fn(eng).then_inc(sem, n)


class Lane:

    def __init__(self, sem):
        self.sem, self.count = sem, 0


class Ring:

    def __init__(self, bufs):
        self.bufs, self.free, self.at = bufs, [() for _ in bufs], -1

    def take(self):
        self.at = (self.at + 1) % len(self.bufs)
        return self.at, self.bufs[self.at], self.free[self.at]

    def give(self, i, *after):
        self.free[i] = after


def build(nc, x, W_inT, conv_w, W_xT, W_dtT, b_dt, A_log, D_param, W_CT, W_outT, gate_wT,
          W1, b1, W2, b2, sW1, sb1, sW2, sb2, cst, sel, tok, out):
    f32, bf16, i32, u32 = mybir.dt.float32, mybir.dt.bfloat16, mybir.dt.int32, mybir.dt.uint32
    ALU, ACT, AX = mybir.AluOpType, mybir.ActivationFunctionType, mybir.AxisListType

    x1_d = nc.dram_tensor("x1_d", [T, D], f32, kind="Internal").ap()
    xn_d = nc.dram_tensor("xn_d", [T, D], f32, kind="Internal").ap()
    sh_d = nc.dram_tensor("sh_d", [T, D], f32, kind="Internal").ap()
    yg_d = nc.dram_tensor("yg_d", [NTILE * ROWS, D], f32, kind="Internal").ap()
    id_d = nc.dram_tensor("id_d", [128 * NCOL, 1], i32, kind="Internal").ap()

    ctx = ExitStack()
    with ctx:
        def sb(name, shape, dt=f32):
            return ctx.enter_context(nc.sbuf_tensor(name, shape, dt))

        def sem(name):
            return ctx.enter_context(nc.semaphore(name))

        lanes = {}

        def lane(name):
            if name not in lanes:
                lanes[name] = Lane(sem("l_" + name))
            return lanes[name]

        q = Queues(sem)
        op, dma = q.op, q.dma

        C = sb("C", [128, CW])
        SEL = sb("SEL", [96, 16, 128], bf16)
        TOK = sb("TOK", [128, NTOK], i32)
        ident, tri, ones = C[:, CI:CI + 128], C[:, CT:CT + 128], C[:, CO:CO + 128]
        iom8, thr, tidx = C[:, CM8:CM8 + 8], C[:, CTH:CTH + 16], C[:, CTI:CTI + NTILE]
        mhalf, eps = C[:, CMH:CMH + 8], C[:, CEP:CEP + 1]
        wxz = sb("wxz", [128, 2, 512])
        wx = sb("wx", [128, 2, 176])
        wdc = sb("wdc", [80, 256])
        wout = sb("wout", [128, 2, 256])
        wg = sb("wg", [128, 2, 8])
        cw = sb("cw", [128, 2, 3])
        bdt = sb("bdt", [128, 2])
        nea = sb("nea", [128, 2, 16])
        Dp = sb("Dp", [128, 2])
        s1 = sb("s1", [128, 2, F])
        s2 = sb("s2", [128, 8, D])
        sb1t = sb("sb1t", [128, 8])
        sb2t = sb("sb2t", [128, D])
        lg = sb("lg", [128, NTOK, 8])
        wts = sb("wts", [128, 2, NTOK])
        pos = sb("pos", [128, 2, NTOK], i32)
        texp = sb("texp", [128, NTILE], i32)
        ids = sb("ids", [128, NCOL], i32)
        stats = sb("stats", [128, 8, 6])
        mv = sb("mv", [128, 8, 2])
        rs = sb("rs", [128, 8])
        nm = sb("nm", [128, 8])
        ARENA = 43012
        arena = sb("arena", [128, ARENA])
        at = [0]

        def cut(n):
            at[0] += n
            assert at[0] <= ARENA, at[0]
            return arena[:, at[0] - n:at[0]]

        PS = [ctx.enter_context(nc.psum_tensor(f"ps{i}", [128, 512], f32)) for i in range(8)]

        def load(dst, src, name="w"):
            return dma("sync", lane(name), lambda e: e.dma_start(dst, src))

        xin = [cut(2048).rearrange("p (j d) -> p j d", j=8) for _ in range(2)]
        xin_free = [(), ()]
        x_t = {}

        def load_x(b):
            x_t[b] = dma("sync", lane(f"x{b % 2}"), lambda e: e.dma_start(
                xin[b % 2], x[b].rearrange("(j p) d -> p j d", p=128)), *xin_free[b % 2])

        load_x(0)
        load(C[:, :], cst)
        load(cw[:, :, :], conv_w.rearrange("(c p) k -> p c k", p=128))
        t_c = load(wxz[:, :, :], W_inT.rearrange("(c p) e -> p c e", p=128))
        z_wx = op("gpsimd", lambda e: e.memset(wx[:, :, :], 0.0))
        wxv = W_xT.rearrange("(c p) e -> p c e", p=128)
        pieces = [(0, 0, 64), (64, 80, 16)] + [(80 + 32 * g, 64, 16) for g in range(3)]
        for to, fr, n in pieces:
            t_wx = dma("sync", lane("wx"), lambda e, to=to, fr=fr, n=n: e.dma_start(
                wx[:, :, to:to + n], wxv[:, :, fr:fr + n]), z_wx)
        load(wdc[0:64, :], W_dtT, "v")
        load(wdc[64:80, :], W_CT, "v")
        load(bdt[:, :], b_dt, "v")
        load(nea[:, :, :], A_log.rearrange("(c p) n -> p c n", p=128), "v")
        load(SEL[:, :, :], sel.rearrange("k (n m) -> k n m", n=16), "v")
        load(Dp[:, :], D_param, "v")
        load(wout[:, :, :], W_outT.rearrange("(c p) e -> p c e", p=128), "v")
        load(wg[:, :, :], gate_wT.rearrange("(c p) e -> p c e", p=128), "v")
        t_v = load(TOK[:, :], tok, "v")
        load(s1[:, :, :], sW1.rearrange("(c p) f -> p c f", p=128), "s")
        load(s2[:, :, :], sW2.rearrange("(c p) h -> p c h", p=128), "s")
        load(sb1t[:, :], sb1, "s")
        t_s = load(sb2t[:, :], sb2.unsqueeze(0).to_broadcast([128, D]), "s")
        load_x(1)
        z_ids = op("gpsimd", lambda e: e.memset(ids[:, :], 0))
        t_id0 = dma("sync", lane("id"), lambda e: e.dma_start(
            id_d.rearrange("(p c) o -> p (c o)", p=128), ids[:, :]), z_ids)
        t_ea = op("scalar", lambda e: e.activation(nea[:, :, :], nea[:, :, :], ACT.Exp), t_v)
        t_nea = op("vector", lambda e: e.tensor_scalar(
            nea[:, :, :], nea[:, :, :], -1.0, None, ALU.mult), t_ea)

        TA = cut(2052)
        TBb = cut(2048)
        xnb = TA[:, 0:2048].rearrange("p (j d) -> p j d", j=8)
        xcp = TA.rearrange("p (c t) -> p c t", c=2)
        btmp = [TA[0:96, 0:1024], TA[0:96, 1024:2048]]
        xnT = TBb.rearrange("p (c t) -> p c t", c=2)
        spt = xnT
        dbl = [[cut(2048).rearrange("p (c t) -> p c t", c=2) for _ in range(2)] for _ in range(3)]
        xs, dts, us = dbl
        zsl = [cut(2048).rearrange("p (j d) -> p j d", j=8) for _ in range(2)]
        dcb = [cut(1024) for _ in range(2)]
        bst = [cut(512).bitcast(bf16) for _ in range(2)]
        ringA = Ring([cut(1024) for _ in range(2)])
        ringB = Ring([cut(1024) for _ in range(2)])
        ringS = Ring([cut(1024) for _ in range(3)])
        PA, PB = cut(2048), cut(2048)
        yb = PA.rearrange("p (c t) -> p c t", c=2)
        gb = PB.rearrange("p (j d) -> p j d", j=8)
        Cs = cut(1024)
        hT = cut(2048).rearrange("p (f t) -> p f t", f=8)
        ringO = Ring([cut(512).rearrange("p (j d) -> p j d", j=2) for _ in range(2)])
        end_a = at[0]

        gen = Ring(PS[6:8])
        bbr = Ring([PS[0:2], PS[2:4]])
        ssum = PS[4:6]

        def layernorm(src, dst, mv_free, *ready, engine="scalar"):
            for j in range(8):
                t = op("vector", lambda e, j=j: e.bn_stats(stats[:, j, :], src(j)), *ready[j])
            for j in range(8):
                t = op("vector", lambda e, j=j: e.bn_aggr(mv[:, j, :], stats[:, j, :]), t, *mv_free)
            t = op("vector", lambda e: e.tensor_scalar(rs[:, :], mv[:, :, 1], eps, None, ALU.add), t)
            t = op("gpsimd", lambda e: e.tensor_tensor(rs[:, :], rs[:, :], mhalf, ALU.pow), t)
            t = op("vector", lambda e: e.scalar_tensor_tensor(
                nm[:, :], mv[:, :, 0], -1.0, rs[:, :], ALU.mult, ALU.mult), t)
            for j in range(8):
                w = op("scalar", lambda e, j=j: e.activation(
                    dst(j), src(j), ACT.Identity, bias=nm[:, j:j + 1], scale=rs[:, j:j + 1]), t)
            return w

        st = {"ln": (), "TA": (), "TB": (), "PA": (), "PB": (), "hT": (), "Cs": ()}
        R = {}

        def transposed(src, dst, after, free):
            w = []
            for c in range(2):
                for h in range(2):
                    i, ps, fr = gen.take()
                    for j in range(4):
                        t = op("tensor", lambda e, j=j, c=c, h=h, ps=ps: e.transpose(
                            ps[:, 128 * j:128 * j + 128], src(4 * h + j)[:, 128 * c:128 * c + 128],
                            ident), t_c, after, *fr)
                    t = op("scalar", lambda e, c=c, h=h, ps=ps: e.copy(
                        dst[:, c, 512 * h:512 * h + 512], ps[:, :]), t, *free)
                    gen.give(i, t)
                    w.append(t)
            return w

        def prep(b):
            p = b % 2
            X = xin[p]
            r = R[b] = {}
            w = layernorm(lambda j: X[:, j, :], lambda j: xnb[:, j, :],
                          st["ln"] + st["TA"], *[(x_t[b], t_c)] * 8)
            st["ln"] = (w,)
            yield
            xt = transposed(lambda j: xnb[:, j, :], xnT, w, st["TB"])
            yield
            a = [op("gpsimd", lambda e: e.memset(xcp[:, :, 0:1], 0.0), *xt),
                 op("gpsimd", lambda e: e.memset(xcp[:, :, 1025:1026], 0.0), *xt)]
            for c in range(2):
                for h in range(2):
                    i, ps, fr = gen.take()
                    for k in range(2):
                        t = op("tensor", lambda e, c=c, h=h, k=k, ps=ps: e.matmul(
                            ps[:, :], wxz[:, k, 128 * c:128 * c + 128],
                            xnT[:, k, 512 * h:512 * h + 512], start=k == 0, stop=k == 1), *xt, *fr)
                    t = op("scalar", lambda e, c=c, h=h, ps=ps: e.copy(
                        xcp[:, c, 1 + 512 * h:513 + 512 * h], ps[:, :]), t)
                    gen.give(i, t)
                    a.append(t)
            yield
            cv = []
            for c in range(2):
                t = op("vector", lambda e, c=c: e.tensor_scalar(
                    xs[p][:, c, :], xcp[:, c, 1:1025], cw[:, c, 1:2], None, ALU.mult), *a, *st.get(f"xs{p}", ()))
                t = op("vector", lambda e, c=c: e.scalar_tensor_tensor(
                    xs[p][:, c, :], xcp[:, c, 0:1024], cw[:, c, 0:1], xs[p][:, c, :], ALU.mult, ALU.add), t)
                t = op("vector", lambda e, c=c: e.scalar_tensor_tensor(
                    xs[p][:, c, :], xcp[:, c, 2:1026], cw[:, c, 2:3], xs[p][:, c, :], ALU.mult, ALU.add), t)
                cv.append(t)
            zt = []
            for g in range(4):
                i, ps, fr = gen.take()
                for j in range(2):
                    for k in range(2):
                        t = op("tensor", lambda e, g=g, j=j, k=k, ps=ps: e.matmul(
                            ps[:, 256 * j:256 * j + 256], xnT[:, k, 128 * (2 * g + j):128 * (2 * g + j) + 128],
                            wxz[:, k, 256:512], start=k == 0, stop=k == 1), *fr)
                z = op("scalar", lambda e, g=g, ps=ps: e.activation(
                    zsl[p][:, 2 * g:2 * g + 2, :], ps[:, :], ACT.Silu), t, *st.get(f"zs{p}", ()))
                gen.give(i, z)
            r["zs"] = z
            st["TB"] = (t,)
            yield
            for c in range(2):
                t_xs = op("scalar", lambda e, c=c: e.activation(
                    xs[p][:, c, :], xs[p][:, c, :], ACT.Silu), cv[c])
            r["xs"] = t_xs
            yield
            bw = []
            for h in range(2):
                i, ps, fr = gen.take()
                for k in range(2):
                    t = op("tensor", lambda e, h=h, k=k, ps=ps: e.matmul(
                        ps[0:80, :], wx[:, k, 0:80], xs[p][:, k, 512 * h:512 * h + 512],
                        start=k == 0, stop=k == 1), t_xs, t_wx, *fr)
                t_dc = op("scalar", lambda e, h=h, ps=ps: e.copy(
                    dcb[p][0:80, 512 * h:512 * h + 512], ps[0:80, :]), t, *st.get(f"dc{p}", ()))
                gen.give(i, t_dc)
                i, ps, fr = gen.take()
                for k in range(2):
                    t = op("tensor", lambda e, h=h, k=k, ps=ps: e.matmul(
                        ps[0:96, :], wx[:, k, 80:176], xs[p][:, k, 512 * h:512 * h + 512],
                        start=k == 0, stop=k == 1), *fr)
                t = op("scalar", lambda e, h=h, ps=ps: e.copy(
                    btmp[0][:, 512 * h:512 * h + 512], ps[0:96, :]), t, *cv)
                gen.give(i, t)
                bw.append(t)
            r["dc"] = t_dc
            yield
            t = op("vector", lambda e: e.tensor_copy(bst[p][0:96, :], btmp[0]), *bw, *st.get(f"bst{p}", ()))
            t = op("vector", lambda e: e.tensor_tensor(btmp[1], btmp[0], bst[p][0:96, :], ALU.subtract), t)
            t1 = op("vector", lambda e: e.tensor_copy(bst[p][0:64, :], btmp[1][0:64, :]), t)
            t = op("vector", lambda e: e.tensor_tensor(
                btmp[0][0:32, :], btmp[1][0:32, :], bst[p][0:32, :], ALU.subtract), t1)
            r["bst"] = op("vector", lambda e: e.tensor_copy(bst[p][0:32, :], btmp[0][0:32, :]), t)
            st["TA"] = (r["bst"],)
            yield
            v, m = [], []
            for c in range(2):
                for h in range(2):
                    i, ps, fr = gen.take()
                    sl = slice(512 * h, 512 * h + 512)
                    t = op("tensor", lambda e, c=c, sl=sl, ps=ps: e.matmul(
                        ps[:, :], wdc[0:64, 128 * c:128 * c + 128], dcb[p][0:64, sl],
                        start=True, stop=True), t_dc, t_v, *fr)
                    u = op("vector", lambda e, c=c, sl=sl, ps=ps: e.tensor_scalar(
                        dts[p][:, c, sl], ps[:, :], bdt[:, c:c + 1], 0.0, ALU.add, ALU.max),
                        t, *st.get(f"dt{p}", ()))
                    a = op("scalar", lambda e, c=c, sl=sl, ps=ps: e.activation(
                        spt[:, c, sl], ps[:, :], ACT.Abs, bias=bdt[:, c:c + 1]), t, u, *st["TB"])
                    gen.give(i, u, a)
                    v.append(a)
                    m.append(u)
            for c in range(2):
                t = op("scalar", lambda e, c=c: e.activation(
                    spt[:, c, :], spt[:, c, :], ACT.Exp, scale=-1.0), *v)
            yield
            for c in range(2):
                t = op("scalar", lambda e, c=c: e.activation(
                    spt[:, c, :], spt[:, c, :], ACT.Ln, bias=1.0), t)
            for c in range(2):
                t2 = op("vector", lambda e, c=c: e.scalar_tensor_tensor(
                    dts[p][:, c, :], spt[:, c, :], 1e-5, dts[p][:, c, :], ALU.add, ALU.add), t, *m)
            r["dt"] = t2
            st["TB"] = (t2,)
            yield
            for c in range(2):
                t = op("gpsimd", lambda e, c=c: e.tensor_tensor(
                    us[p][:, c, :], dts[p][:, c, :], xs[p][:, c, :], ALU.mult), t2, r["xs"], *st.get(f"u{p}", ()))
            r["u"] = t
            yield

        def main(b):
            p, r = b % 2, R[b]
            nxt = {}

            def spread(k):
                i, bb, fr = bbr.take()
                for h in range(2):
                    t = op("tensor", lambda e, h=h, bb=bb, n=k % 16: e.matmul(
                        bb[h][:, :], SEL[:, n, :], bst[p][0:96, 512 * h:512 * h + 512],
                        start=True, stop=True), r["bst"], t_v, *fr)
                nxt[k] = (i, bb, t)

            spread(0)
            late = None
            for c in range(2):
                for n in range(16):
                    k = 16 * c + n
                    if k < 31:
                        spread(k + 1)
                    ia, A, fa = ringA.take()
                    t_a = op("scalar", lambda e, A=A, c=c, n=n: e.activation(
                        A, dts[p][:, c, :], ACT.Exp, scale=nea[:, c, n:n + 1]), r["dt"], t_nea, *fa)
                    i, bb, t_b = nxt[k]
                    ib, Bx, fb = ringB.take()
                    for h in range(2):
                        t = op("vector", lambda e, h=h, bb=bb, Bx=Bx, c=c: e.tensor_tensor(
                            Bx[:, 512 * h:512 * h + 512], us[p][:, c, 512 * h:512 * h + 512],
                            bb[h][:, :], ALU.mult), t_b, r["u"], *fb)
                    bbr.give(i, t)
                    is_, S, fs = ringS.take()
                    t_sc = op("vector", lambda e, A=A, Bx=Bx, S=S: e.tensor_tensor_scan(
                        S, A, Bx, 0.0, ALU.mult, ALU.add), t_a, t, *fs)
                    ringA.give(ia, t_sc)
                    ringB.give(ib, t_sc)
                    free = st.get("ssum", ()) if n == 0 else ()

                    def add(S=S, n=n, is_=is_, t_sc=t_sc, free=free):
                        for h in range(2):
                            t = op("tensor", lambda e, h=h: e.matmul(
                                ssum[h][:, :], ident, S[:, 512 * h:512 * h + 512],
                                start=n == 0, stop=n == 15), t_sc, *free)
                        ringS.give(is_, t)
                        return t
                    t_sum = add()
                    if n == 4:
                        for h in range(2):
                            i2, ps, fr = gen.take()
                            sl = slice(512 * h, 512 * h + 512)
                            t = op("tensor", lambda e, c=c, sl=sl, ps=ps: e.matmul(
                                ps[:, :], wdc[64:80, 128 * c:128 * c + 128], dcb[p][64:80, sl],
                                start=True, stop=True), r["dc"], *fr)
                            t_cs = op("scalar", lambda e, sl=sl, ps=ps: e.copy(
                                Cs[:, sl], ps[:, :]), t, *st["Cs"])
                            gen.give(i2, t_cs)
                            st[f"dc{p}"] = (t,)
                    if n < 15:
                        yield
                for h in range(2):
                    sl = slice(512 * h, 512 * h + 512)
                    t = op("vector", lambda e, sl=sl, c=c, h=h: e.tensor_tensor(
                        yb[:, c, sl], Cs[:, sl], ssum[h][:, :], ALU.mult), t_sum, t_cs, *st["PA"])
                st["ssum"] = (t,)
                st["Cs"] = (t,)
                t = op("vector", lambda e, c=c: e.scalar_tensor_tensor(
                    yb[:, c, :], xs[p][:, c, :], Dp[:, c:c + 1], yb[:, c, :], ALU.mult, ALU.add), t, r["xs"])
                if c == 1:
                    r["y"] = t
                    st[f"xs{p}"] = (t, r["u"])
                    st[f"dt{p}"] = (t_a, r["u"])
                    st[f"u{p}"] = (t_sc,)
                    st[f"bst{p}"] = (t_b,)
                yield

        def post(b):
            p, r = b % 2, R[b]
            X = xin[p]
            gt = []
            for g in range(4):
                i, ps, fr = gen.take()
                for j in range(2):
                    for k in range(2):
                        t = op("tensor", lambda e, g=g, j=j, k=k, ps=ps: e.matmul(
                            ps[:, 256 * j:256 * j + 256], yb[:, k, 128 * (2 * g + j):128 * (2 * g + j) + 128],
                            wout[:, k, :], start=k == 0, stop=k == 1), r["y"], *fr)
                t_y = t
                t = op("vector", lambda e, g=g, ps=ps: e.tensor_tensor(
                    gb[:, 2 * g:2 * g + 2, :], zsl[p][:, 2 * g:2 * g + 2, :],
                    ps[:, :].rearrange("p (j d) -> p j d", j=2), ALU.mult), t, r["zs"], *st["PB"])
                gen.give(i, t)
                gt += [t, t]
                if g % 2:
                    yield
            st[f"zs{p}"] = (t,)
            w = layernorm(lambda j: gb[:, j, :], lambda j: gb[:, j, :], st["ln"], *[(t,) for t in gt])
            st["ln"] = (w,)
            yield
            t = op("gpsimd", lambda e: e.tensor_tensor(X[:, :, :], X[:, :, :], gb[:, :, :], ALU.add), w, x_t[b])
            o1 = dma("sync", lane(f"x1{p}"), lambda e: e.dma_start(
                x1_d[TB * b:TB * (b + 1), :].rearrange("(j p) d -> p j d", p=128), X[:, :, :]), t)
            yield
            w = layernorm(lambda j: X[:, j, :], lambda j: gb[:, j, :], st["ln"], *[(t,)] * 8)
            st["ln"] = (w,)
            o2 = dma("sync", lane(f"xn{p}"), lambda e: e.dma_start(
                xn_d[TB * b:TB * (b + 1), :].rearrange("(j p) d -> p j d", p=128), gb[:, :, :]), w)
            r["stored"] = (o1, o2)
            xin_free[p] = (o1, w)
            if b + 2 < NB:
                load_x(b + 2)
            yield
            xt = transposed(lambda j: gb[:, j, :], yb, w, (t_y,))
            st["PB"] = (o2, xt[-1])
            i, ps, fr = gen.take()
            for j in range(8):
                for k in range(2):
                    t = op("tensor", lambda e, j=j, k=k, ps=ps: e.matmul(
                        ps[:, 8 * j:8 * j + 8], yb[:, k, 128 * j:128 * j + 128], wg[:, k, :],
                        start=k == 0, stop=k == 1), *xt, *fr)
            t = op("scalar", lambda e, ps=ps: e.copy(
                lg[:, 8 * b:8 * b + 8, :], ps[:, 0:64].rearrange("p (j e) -> p j e", j=8)), t)
            gen.give(i, t)
            r["lg"] = t
            yield
            for g in range(4):
                hw = []
                for f in range(0, 8, 2):
                    i, ps, fr = gen.take()
                    for a in range(2):
                        for k in range(2):
                            t = op("tensor", lambda e, f=f + a, a=a, k=k, g=g, ps=ps: e.matmul(
                                ps[:, 256 * a:256 * a + 256], s1[:, k, 128 * f:128 * f + 128],
                                yb[:, k, 256 * g:256 * g + 256], start=k == 0, stop=k == 1), t_s, *xt, *fr)
                    for a in range(2):
                        t = op("scalar", lambda e, f=f + a, a=a, ps=ps: e.activation(
                            hT[:, f, :], ps[:, 256 * a:256 * a + 256], ACT.Gelu, bias=sb1t[:, f:f + 1]),
                            t, *st["hT"])
                        hw.append(t)
                    gen.give(i, t)
                    t_xt = t
                yield
                i, ps, fr = gen.take()
                for j in range(2):
                    for f in range(8):
                        t = op("tensor", lambda e, j=j, f=f, ps=ps: e.matmul(
                            ps[:, 256 * j:256 * j + 256], hT[:, f, 128 * j:128 * j + 128], s2[:, f, :],
                            start=f == 0, stop=f == 7), hw[f], *fr)
                st["hT"] = (t,)
                io, O, fo = ringO.take()
                for j in range(2):
                    t2 = op("vector", lambda e, j=j, ps=ps, O=O: e.tensor_tensor(
                        O[:, j, :], sb2t[:, :], ps[:, 256 * j:256 * j + 256], ALU.add), t, t_s, *fo)
                gen.give(i, t2)
                o = dma("sync", lane(f"sh{io}"), lambda e, g=g, O=O: e.dma_start(
                    sh_d[TB * b + 256 * g:TB * b + 256 * g + 256, :].rearrange("(j p) d -> p j d", p=128), O), t2)
                ringO.give(io, o)
                r.setdefault("sh", []).append(o)
                yield
            st["PA"] = (t_xt,)

        def chain(*gens):
            for g in gens:
                yield from g

        for _ in prep(0):
            pass
        for b in range(NB):
            side = chain(post(b - 1) if b else iter(()), prep(b + 1) if b + 1 < NB else iter(()))
            for _ in main(b):
                next(side, None)
            for _ in side:
                pass
        for _ in post(NB - 1):
            pass

        at[0] = 0
        last = [(q.sems[e], q.count[e], e) for e in q.ENGINES if q.count[e]]
        for b in range(NB):
            last += list(R[b]["stored"]) + R[b]["sh"]
        rb = cut(256 * 12)
        at3 = [0]

        def r3(n=256):
            at3[0] += n
            return rb[:, at3[0] - n:at3[0]]

        def v3(a):
            return a.rearrange("p (j e) -> p j e", e=8)

        def over_e(a):
            return a.unsqueeze(2).to_broadcast([128, NTOK, 8])

        def over_j(a):
            return a.unsqueeze(1).to_broadcast([128, NTOK, 8])

        pr, oh1, oh2, eq, M, pre, tot, inc = (r3() for _ in range(8))
        mx, z, ix, m1, m2, cnt = (r3(32) for _ in range(6))
        nt, ts, te, bs = (r3(8) for _ in range(4))
        ntb = r3(128)
        assert at3[0] <= 256 * 12
        te8 = cut(NTILE * 8)
        texf = cut(NTILE)
        qi, pi = cut(64).bitcast(i32), cut(64).bitcast(i32)
        posf = cut(64)

        def dve(fn, *after):
            return op("vector", fn, *after)

        t = dve(lambda e: e.reduce_max(mx, lg[:, :, :], axis=AX.X), *last)
        t = dve(lambda e: e.tensor_tensor(v3(pr), lg[:, :, :], over_e(mx), ALU.subtract), t)
        t = op("scalar", lambda e: e.activation(pr, pr, ACT.Exp), t)
        t = dve(lambda e: e.reduce_sum(z, v3(pr), axis=AX.X), t)
        t = dve(lambda e: e.reciprocal(z, z), t)
        t = dve(lambda e: e.tensor_tensor(v3(pr), v3(pr), over_e(z), ALU.mult), t)

        def best(oh, m, t):
            t = dve(lambda e: e.reduce_max(m, v3(pr), axis=AX.X), t)
            t = dve(lambda e: e.tensor_tensor(v3(eq), v3(pr), over_e(m), ALU.is_equal), t)
            t = dve(lambda e: e.tensor_tensor(v3(eq), v3(eq), over_j(iom8), ALU.mult), t)
            t = dve(lambda e: e.tensor_reduce(ix, v3(eq), axis=AX.X, op=ALU.min), t)
            return dve(lambda e: e.tensor_tensor(v3(oh), over_e(ix), over_j(iom8), ALU.is_equal), t)

        t = best(oh1, m1, t)
        t = dve(lambda e: e.scalar_tensor_tensor(pr, oh1, -2.0, pr, ALU.mult, ALU.add), t)
        t = best(oh2, m2, t)
        t_m = dve(lambda e: e.tensor_tensor(M, oh1, oh2, ALU.add), t)
        t = dve(lambda e: e.tensor_tensor(z, m1, m2, ALU.add), t_m)
        t = dve(lambda e: e.reciprocal(z, z), t)
        dve(lambda e: e.tensor_tensor(wts[:, 0, :], m1, z, ALU.mult), t)
        t_w = dve(lambda e: e.tensor_tensor(wts[:, 1, :], m2, z, ALU.mult), t)
        op("tensor", lambda e: e.matmul(PS[0][:, 0:256], tri, M, start=True, stop=True), t_m, *last)
        t = op("tensor", lambda e: e.matmul(PS[1][:, 0:256], ones, M, start=True, stop=True), t_m)
        t = dve(lambda e: e.tensor_copy(pre, PS[0][:, 0:256]), t)
        t = dve(lambda e: e.tensor_copy(tot, PS[1][:, 0:256]), t)
        for x8 in range(8):
            t2 = dve(lambda e, x8=x8: e.tensor_tensor_scan(
                v3(inc)[:, :, x8], ones[:, 0:NTOK], v3(tot)[:, :, x8], 0.0, ALU.mult, ALU.add), t)
        t = dve(lambda e: e.tensor_copy(cnt[:, 0:8], v3(inc)[:, NTOK - 1, :]), t2)
        nt3 = ntb.rearrange("p (e i) -> p e i", i=16)
        t = dve(lambda e: e.tensor_tensor(nt3, cnt[:, 0:8].unsqueeze(2).to_broadcast([128, 8, 16]),
                                          thr.unsqueeze(1).to_broadcast([128, 8, 16]), ALU.is_gt), t)
        t = dve(lambda e: e.reduce_sum(nt, nt3, axis=AX.X), t)
        t = dve(lambda e: e.tensor_tensor_scan(te, ones[:, 0:8], nt, 0.0, ALU.mult, ALU.add), t)
        t_te = t
        t = dve(lambda e: e.tensor_tensor(ts, te, nt, ALU.subtract), t)
        t = dve(lambda e: e.tensor_scalar(bs, ts, float(ROWS), None, ALU.mult), t)
        te3 = te8.rearrange("p (i e) -> p i e", e=8)
        t8 = dve(lambda e: e.tensor_tensor(te3, tidx.unsqueeze(2).to_broadcast([128, NTILE, 8]),
                                           te.unsqueeze(1).to_broadcast([128, NTILE, 8]), ALU.is_ge), t_te)
        t8 = dve(lambda e: e.reduce_sum(texf, te3, axis=AX.X), t8)
        t_ex = dve(lambda e: e.tensor_scalar(texp[:, :], texf, 7.0, None, ALU.min), t8)
        t = dve(lambda e: e.tensor_tensor(pre, pre, inc, ALU.add), t)
        t = dve(lambda e: e.tensor_tensor(pre, pre, tot, ALU.subtract), t)
        t = dve(lambda e: e.tensor_tensor(v3(pre), v3(pre), over_j(bs), ALU.add), t)
        for k, oh in enumerate((oh1, oh2)):
            t1 = dve(lambda e, oh=oh: e.tensor_tensor(oh, oh, pre, ALU.mult), t)
            t1 = dve(lambda e, k=k, oh=oh: e.reduce_sum(posf[:, 32 * k:32 * k + 32], v3(oh), axis=AX.X), t1)
        posv = pos[:, :, :].rearrange("p k j -> p (k j)")
        t_pos = dve(lambda e: e.tensor_copy(posv, posf), t1)
        t = dve(lambda e: e.tensor_scalar(qi, posv, 7, None, ALU.logical_shift_right), t_pos)
        t = dve(lambda e: e.tensor_scalar(pi, posv, 127, None, ALU.bitwise_and), t)
        t = dve(lambda e: e.scalar_tensor_tensor(qi, pi, float(NCOL), qi, ALU.mult, ALU.add), t)
        for k in range(2):
            for j in range(NTOK):
                t2 = dma("gpsimd", lane("scat"), lambda e, k=k, j=j: e.indirect_dma_start(
                    id_d, bass.IndirectOffsetOnAxis(ap=qi.bitcast(u32)[:, 32 * k + j:32 * k + j + 1], axis=0),
                    TOK[:, j:j + 1], None), t, t_v, t_id0)
        t_ids = dma("sync", lane("ids"), lambda e: e.dma_start(
            ids[:, :], id_d.rearrange("(p c) o -> p (c o)", p=128)), t2, t_id0)

        w1v = W1.rearrange("e (c p) f -> e p c f", p=128)
        w2v = W2.rearrange("e (c p) h -> e p c h", p=128)
        NW = 3
        ringW = Ring([(cut(2048).rearrange("p (c f) -> p c f", c=2),
                       cut(2048).rearrange("p (c h) -> p c h", c=8), cut(8), cut(256)) for _ in range(NW)])
        ringG = Ring([cut(512).rearrange("p (j d) -> p j d", j=2) for _ in range(4)])
        ringX = Ring([cut(512).rearrange("p (c t) -> p c t", c=2) for _ in range(2)])
        ringH = Ring([cut(2048).rearrange("p (f t) -> p f t", f=8) for _ in range(2)])
        ringY = Ring([cut(512).rearrange("p (j d) -> p j d", j=2) for _ in range(3)])
        pX, pH, pY = Ring(PS[0:2]), Ring(PS[2:6]), Ring(PS[6:8])
        first = last
        regs = {}

        def read(i):
            def fn(e):
                regs[i] = e.value_load(texp[0:1, i:i + 1], min_val=0, max_val=E - 1)
                return e.dma_start(Ws[i][1][0], w1v[bass.ds(regs[i], 1)].squeeze(0))
            return fn

        def part(i, n, src):
            return lambda e: e.dma_start(Ws[i][1][n], src(regs[i]))

        Ws, G = {}, {}

        def weights(i):
            iw, W, fw = ringW.take()
            Ws[i] = (iw, W)
            ln = lane(f"W{iw}")
            dma("sync", ln, read(i), t_ex, *fw, *first)
            dma("sync", ln, part(i, 1, lambda v: w2v[bass.ds(v, 1)].squeeze(0)))
            dma("sync", ln, part(i, 2, lambda v: b1[bass.ds(v, 1)].squeeze(0)))
            Ws[i] += (dma("sync", ln, part(i, 3, lambda v: b2[bass.ds(v, 1)].to_broadcast([128, D]))),)

        def gather(i):
            ig, g, fg = ringG.take()
            for j in range(2):
                t = dma("gpsimd", lane(f"G{ig}"), lambda e, g=g, j=j: e.indirect_dma_start(
                    g[:, j, :], None, xn_d,
                    bass.IndirectOffsetOnAxis(ap=ids[:, 2 * i + j:2 * i + j + 1].bitcast(u32), axis=0)),
                    t_ids, *fg, *first)
            G[i] = (ig, g, t)

        for i in range(min(NW, NTILE)):
            weights(i)
        for i in range(4):
            gather(i)
        yst = []
        for i in range(NTILE):
            ig, g, t_g = G[i]
            iw, (w1, w2, bb1, bb2), t_wt = Ws[i]
            ix_, ps, fr = pX.take()
            for c in range(2):
                for j in range(2):
                    t = op("tensor", lambda e, c=c, j=j, ps=ps, g=g: e.transpose(
                        ps[:, 256 * c + 128 * j:256 * c + 128 * j + 128], g[:, j, 128 * c:128 * c + 128],
                        ident), t_g, *fr)
            ringG.give(ig, t)
            ixs, xT, fx = ringX.take()
            t_x = op("vector", lambda e, ps=ps, xT=xT: e.tensor_copy(
                xT, ps[:, :].rearrange("p (c t) -> p c t", c=2)), t, *fx)
            pX.give(ix_, t_x)
            ih, h, fh = ringH.take()
            hw = []
            for f in range(0, 8, 2):
                ip, ps, fr = pH.take()
                for a in range(2):
                    for k in range(2):
                        t = op("tensor", lambda e, f=f + a, a=a, k=k, ps=ps, w1=w1, xT=xT: e.matmul(
                            ps[:, 256 * a:256 * a + 256], w1[:, k, 128 * f:128 * f + 128], xT[:, k, :],
                            start=k == 0, stop=k == 1), t_x, t_wt, *fr)
                for a in range(2):
                    t2 = op("scalar", lambda e, f=f + a, a=a, ps=ps, h=h, bb1=bb1: e.activation(
                        h[:, f, :], ps[:, 256 * a:256 * a + 256], ACT.Gelu, bias=bb1[:, f:f + 1]), t, t_wt, *fh)
                    hw.append(t2)
                pH.give(ip, t2)
            ringX.give(ixs, t)
            ip, ps, fr = pY.take()
            for j in range(2):
                for f in range(8):
                    t = op("tensor", lambda e, j=j, f=f, ps=ps, h=h, w2=w2: e.matmul(
                        ps[:, 256 * j:256 * j + 256], h[:, f, 128 * j:128 * j + 128], w2[:, f, :],
                        start=f == 0, stop=f == 7), hw[f], *fr)
            ringH.give(ih, t)
            iy, y, fy = ringY.take()
            for j in range(2):
                t2 = op("vector", lambda e, j=j, ps=ps, y=y, bb2=bb2: e.tensor_tensor(
                    y[:, j, :], bb2, ps[:, 256 * j:256 * j + 256], ALU.add), t, t_wt, *fy)
            pY.give(ip, t2)
            ringW.give(iw, t2, t)
            o = dma("scalar", lane(f"Y{iy}"), lambda e, i=i, y=y: e.dma_start(
                yg_d[ROWS * i:ROWS * (i + 1), :].rearrange("(j p) d -> p j d", p=128), y), t2)
            ringY.give(iy, o)
            yst = (yst + [o])[-3:]
            if i + NW < NTILE:
                weights(i + NW)
            if i + 4 < NTILE:
                gather(i + 4)

        def eight(n=2048):
            return cut(n).rearrange("p (j d) -> p j d", j=8)

        pool_bufs = [(eight(), eight()) for _ in range(2)]
        ringL = Ring(pool_bufs)
        gk = Ring([(cut(256), cut(256)) for _ in range(6)])
        outs = []
        for b in range(NB):
            il, (X, S), fl = ringL.take()
            rows = slice(TB * b, TB * (b + 1))
            dma("sync", lane(f"L{il}"), lambda e, rows=rows, S=S: e.dma_start(
                S, sh_d[rows, :].rearrange("(j p) d -> p j d", p=128)), *first, *fl)
            t_l = dma("sync", lane(f"L{il}"), lambda e, rows=rows, X=X: e.dma_start(
                X, x1_d[rows, :].rearrange("(j p) d -> p j d", p=128)), *first, *fl)
            sw = []
            for j in range(8):
                n = 8 * b + j
                ik, (g1, g2), fk = gk.take()
                for k, g in enumerate((g1, g2)):
                    t = dma("gpsimd", lane(f"K{ik}"), lambda e, k=k, g=g, n=n: e.indirect_dma_start(
                        g, None, yg_d,
                        bass.IndirectOffsetOnAxis(ap=pos[:, k, n:n + 1].bitcast(u32), axis=0)),
                        t_pos, *yst, *fk)
                t = dve(lambda e, j=j, n=n, S=S, g1=g1: e.scalar_tensor_tensor(
                    S[:, j, :], g1, wts[:, 0, n:n + 1], S[:, j, :], ALU.mult, ALU.add), t, t_l, t_w)
                t = dve(lambda e, j=j, n=n, S=S, g2=g2: e.scalar_tensor_tensor(
                    S[:, j, :], g2, wts[:, 1, n:n + 1], S[:, j, :], ALU.mult, ALU.add), t)
                gk.give(ik, t)
                sw.append((t,))
            w = layernorm(lambda j, S=S: S[:, j, :], lambda j, S=S: S[:, j, :], st["ln"], *sw)
            st["ln"] = (w,)
            t = dve(lambda e, X=X, S=S: e.tensor_tensor(X, X, S, ALU.add), w, t_l)
            o = dma("sync", lane(f"out{il}"), lambda e, b=b, X=X: e.dma_start(
                out[b].rearrange("(j p) d -> p j d", p=128), X), t)
            ringL.give(il, o)
            outs.append(o)

        block = ctx.enter_context(nc.Block())

        @block.tensor
        def _(eng):
            q.play("tensor", eng)

        @block.vector
        def _(eng):
            q.play("vector", eng)

        @block.scalar
        def _(eng):
            q.play("scalar", eng)

        @block.gpsimd
        def _(eng):
            q.play("gpsimd", eng)

        @block.sync
        def _(eng):
            q.play("sync", eng)
            for ln in lanes.values():
                eng.wait_ge(ln.sem, ln.count)


def kernel(**inputs):
    import numpy as np
    import concourse.bacc as bacc
    from concourse import mybir as mb
    from concourse.bass_utils import run_bass_kernel_spmd as run
    import ml_dtypes

    def a(name):
        return np.ascontiguousarray(inputs[name])

    def t(name):
        return np.ascontiguousarray(np.asarray(inputs[name]).T)

    def cols(name):
        return np.ascontiguousarray(np.asarray(inputs[name]).reshape(-1, 128).T)

    cst = np.zeros((128, CW), np.float32)
    cst[:, CI:CI + 128] = np.eye(128)
    cst[:, CT:CT + 128] = np.triu(np.ones((128, 128)), 1)
    cst[:, CO:CO + 128] = 1.0
    cst[:, CM8:CM8 + 8] = np.arange(8) - 8.0
    cst[:, CTH:CTH + 16] = np.arange(16) * float(ROWS)
    cst[:, CTI:CTI + NTILE] = np.arange(NTILE)
    cst[:, CMH:CMH + 8] = -0.5
    cst[:, CEP] = 1e-5
    sel = np.zeros((96, 16, 128), ml_dtypes.bfloat16)
    for g in range(3):
        for n in range(16):
            sel[32 * g + n, n, :] = 1.0
    tok = (np.arange(NTOK)[None, :] * 128 + np.arange(128)[:, None]).astype(np.int32)
    A, Fp = "L0_attn_", "L0_ffn_"
    arrays = {
        "x": a(A + "x"), "W_inT": t(A + "W_in"), "conv_w": a(A + "conv_w"), "W_xT": t(A + "W_x"),
        "W_dtT": t(A + "W_dt"), "b_dt": cols("L0_attn_b_dt"), "A_log": a(A + "A_log"), "D_param": cols("L0_attn_D_param"),
        "W_CT": t(A + "W_C"), "W_outT": t(A + "W_out"), "gate_wT": t(Fp + "gate_w"),
        "W1": a(Fp + "W1"),
        "b1": np.ascontiguousarray(np.asarray(inputs[Fp + "b1"]).reshape(E, 8, 128).transpose(0, 2, 1)),
        "W2": a(Fp + "W2"), "b2": a(Fp + "b2"), "sW1": a(Fp + "sW1"),
        "sb1": cols("L0_ffn_sb1"),
        "sW2": a(Fp + "sW2"), "sb2": a(Fp + "sb2"),
        "cst": cst, "sel": sel.reshape(96, 2048), "tok": tok,
    }
    nc = bacc.Bacc("TRN2", target_bir_lowering=False, num_devices=1)
    aps = {n: nc.dram_tensor(n, v.shape, mb.dt.from_np(v.dtype), kind="ExternalInput").ap()
           for n, v in arrays.items()}
    out = nc.dram_tensor("out", (NB, TB, D), mb.dt.float32, kind="ExternalOutput").ap()
    build(nc, out=out, **aps)
    r = run(nc, [arrays], core_ids=[0])
    return r.results[0]["out"]
```

```python
import concourse.bass as bass
from concourse import mybir
from contextlib import ExitStack

T, D, F, E, NB, TB = 4096, 256, 1024, 8, 4, 1024
NTOK = T // 128
ROWS = 256
NTILE = (2 * T + E * (ROWS - 1)) // ROWS
NCOL = NTILE * ROWS // 128
CI, CT, CO, CM8, CTH, CTI, CMH, CEP, CP, CR, CV = 0, 128, 256, 384, 392, 408, 448, 456, 457, 458, 586
CW = 650


class Queues:

    ENGINES = ("tensor", "vector", "scalar", "gpsimd", "sync")

    def __init__(self, sem):
        self.items = {e: [] for e in self.ENGINES}
        self.sems = {e: sem("s_" + e) for e in self.ENGINES}
        self.count = {e: 0 for e in self.ENGINES}

    def op(self, engine, fn, *after):
        self.count[engine] += 1
        self.items[engine].append((fn, after, self.sems[engine], 1))
        return (self.sems[engine], self.count[engine], engine)

    def dma(self, engine, lane, fn, *after):
        lane.count += 16
        self.items[engine].append((fn, after, lane.sem, 16))
        return (lane.sem, lane.count, lane.sem)

    def play(self, engine, eng):
        seen = {}
        for fn, after, sem, n in self.items[engine]:
            for s, value, key in after:
                if seen.get(key, 0) < value:
                    eng.wait_ge(s, value)
                    seen[key] = value
            fn(eng).then_inc(sem, n)


class Lane:

    def __init__(self, sem):
        self.sem, self.count = sem, 0


class Ring:

    def __init__(self, bufs):
        self.bufs, self.free, self.at = bufs, [() for _ in bufs], -1
        self.held = set()

    def take(self):
        assert len(self.held) < len(self.bufs)
        self.at = (self.at + 1) % len(self.bufs)
        while self.at in self.held:
            self.at = (self.at + 1) % len(self.bufs)
        self.held.add(self.at)
        return self.at, self.bufs[self.at], self.free[self.at]

    def give(self, i, *after):
        self.held.discard(i)
        self.free[i] = after


def build(nc, x, W_inT, conv_w, W_xT, W_dtT, b_dt, A_log, D_param, W_CT, W_outT, gate_wT,
          W1, b1, W2, b2, sW1, sb1, sW2, sb2, cst, sel, out):
    f32, bf16, i32, u32 = mybir.dt.float32, mybir.dt.bfloat16, mybir.dt.int32, mybir.dt.uint32
    ALU, ACT, AX = mybir.AluOpType, mybir.ActivationFunctionType, mybir.AxisListType

    x1_d = nc.dram_tensor("x1_d", [T, D], f32, kind="Internal").ap()
    xn_d = nc.dram_tensor("xn_d", [T, D], f32, kind="Internal").ap()
    sh_d = nc.dram_tensor("sh_d", [T, D], f32, kind="Internal").ap()
    z_d = nc.dram_tensor("z_d", [2 * T, D], f32, kind="Internal").ap()

    ctx = ExitStack()
    with ctx:
        def sb(name, shape, dt=f32):
            return ctx.enter_context(nc.sbuf_tensor(name, shape, dt))

        def sem(name):
            return ctx.enter_context(nc.semaphore(name))

        lanes = {}

        def lane(name):
            if name not in lanes:
                lanes[name] = Lane(sem("l_" + name))
            return lanes[name]

        q = Queues(sem)
        op, dma = q.op, q.dma

        C = sb("C", [128, CW])
        SEL = sb("SEL", [96, 16], bf16)
        ident, tri, ones = C[:, CI:CI + 128], C[:, CT:CT + 128], C[:, CO:CO + 128]
        iom8, thr, tidx = C[:, CM8:CM8 + 8], C[:, CTH:CTH + 16], C[:, CTI:CTI + NTILE]
        mhalf, eps, prow = C[:, CMH:CMH + 8], C[:, CEP:CEP + 1], C[:, CP:CP + 1]
        i128, vtok = C[:, CR:CR + 128], C[:, CV:CV + 64]
        wxz = sb("wxz", [128, 2, 512])
        wx = sb("wx", [128, 2, 176])
        wdc = sb("wdc", [80, 256])
        wout = sb("wout", [128, 2, 256])
        wg = sb("wg", [128, 2, 8])
        cw = sb("cw", [128, 2, 3])
        bdt = sb("bdt", [128, 2])
        nea = sb("nea", [128, 2, 16])
        Dp = sb("Dp", [128, 2])
        s1 = sb("s1", [128, 2, F])
        s2 = sb("s2", [128, 8, D])
        sb1t = sb("sb1t", [128, 8])
        sb2t = sb("sb2t", [128, D])
        lg = sb("lg", [128, NTOK, 8])
        wts = sb("wts", [128, 2, NTOK])
        texp = sb("texp", [128, NTILE], i32)
        idg = sb("idg", [128, NCOL], i32)
        ids = sb("ids", [128, NCOL], i32)
        stats = sb("stats", [128, 8, 6])
        mv = sb("mv", [128, 8, 2])
        rs = sb("rs", [128, 8])
        nm = sb("nm", [128, 8])
        ARENA = 45060
        arena = sb("arena", [128, ARENA])
        at = [0]

        def cut(n):
            at[0] += n
            assert at[0] <= ARENA, at[0]
            return arena[:, at[0] - n:at[0]]

        PS = [ctx.enter_context(nc.psum_tensor(f"ps{i}", [128, 512], f32)) for i in range(8)]

        def load(dst, src, name="w"):
            return dma("sync", lane(name), lambda e: e.dma_start(dst, src))

        def rows8(a):
            return a.rearrange("(j p) d -> p j d", p=128)

        nT = cut(2048).rearrange("p (c t) -> p c t", c=2)
        hT = cut(2048).rearrange("p (f t) -> p f t", f=8)
        ringO = Ring([cut(512).rearrange("p (j d) -> p j d", j=2) for _ in range(2)])
        kept = at[0]
        X = cut(2048).rearrange("p (j d) -> p j d", j=8)
        TA = cut(2052)
        TBb = cut(2048)
        xnb = TA[:, 0:2048].rearrange("p (j d) -> p j d", j=8)
        xcp = TA.rearrange("p (c t) -> p c t", c=2)
        btmp = [TA[0:96, 0:1024], TA[0:96, 1024:2048]]
        xnT = TBb.rearrange("p (c t) -> p c t", c=2)
        spt = xnT
        dbl = [[cut(2048).rearrange("p (c t) -> p c t", c=2) for _ in range(2)] for _ in range(3)]
        xs, dts, us = dbl
        zsl = [cut(2048).rearrange("p (j d) -> p j d", j=8) for _ in range(2)]
        dcb = [cut(1024) for _ in range(2)]
        bst = [cut(512).bitcast(bf16) for _ in range(2)]
        ringA = Ring([cut(1024) for _ in range(2)])
        ringB = Ring([cut(1024) for _ in range(2)])
        ringS = Ring([cut(1024) for _ in range(5)])
        PA, PB = cut(2048), cut(2048)
        yb = PA.rearrange("p (c t) -> p c t", c=2)
        gb = PB.rearrange("p (j d) -> p j d", j=8)
        Cs = cut(1024)

        gen = Ring(PS[6:8])
        bbr = Ring([PS[0:2], PS[2:4]])
        ssum = PS[4:6]

        st = {"ln": (), "TA": (), "TB": (), "PA": (), "PB": (), "hT": (), "Cs": (), "X": (), "nT": ()}
        R = {}
        x_t = {}

        def load_x(b):
            for h in range(4):
                x_t[b, h] = dma("sync", lane(f"x{h}"), lambda e, h=h: e.dma_start(
                    xnb[:, 2 * h:2 * h + 2, :], rows8(x[b])[:, 2 * h:2 * h + 2, :]), *st["TA"])

        load_x(0)
        load(C[:, :], cst)
        load(cw[:, :, :], conv_w.rearrange("(c p) k -> p c k", p=128))
        t_c = load(wxz[:, :, :], W_inT.rearrange("(c p) e -> p c e", p=128))
        z_wx = op("gpsimd", lambda e: e.memset(wx[:, :, :], 0.0))
        wxv = W_xT.rearrange("(c p) e -> p c e", p=128)
        pieces = [(0, 0, 64), (64, 80, 16)] + [(80 + 32 * g, 64, 16) for g in range(3)]
        for to, fr, n in pieces:
            t_wx = dma("sync", lane("wx"), lambda e, to=to, fr=fr, n=n: e.dma_start(
                wx[:, :, to:to + n], wxv[:, :, fr:fr + n]), z_wx)
        load(wdc[0:64, :], W_dtT, "v")
        load(wdc[64:80, :], W_CT, "v")
        load(bdt[:, :], b_dt, "v")
        load(nea[:, :, :], A_log.rearrange("(c p) n -> p c n", p=128), "v")
        load(SEL[:, :], sel, "v")
        load(Dp[:, :], D_param, "v")
        load(wout[:, :, :], W_outT.rearrange("(c p) e -> p c e", p=128), "v")
        t_v = load(wg[:, :, :], gate_wT.rearrange("(c p) e -> p c e", p=128), "v")
        load(s1[:, :, :], sW1.rearrange("(c p) f -> p c f", p=128), "s")
        load(s2[:, :, :], sW2.rearrange("(c p) h -> p c h", p=128), "s")
        load(sb1t[:, :], sb1, "s")
        t_s = load(sb2t[:, :], sb2.unsqueeze(0).to_broadcast([128, D]), "s")
        t_ea = op("scalar", lambda e: e.activation(nea[:, :, :], nea[:, :, :], ACT.Exp), t_v)
        t_nea = op("vector", lambda e: e.tensor_scalar(
            nea[:, :, :], nea[:, :, :], -1.0, None, ALU.mult), t_ea)

        def layernorm(src, dst, *ready):
            for j in range(8):
                t = op("vector", lambda e, j=j: e.bn_stats(stats[:, j, :], src(j)), *ready[j])
            for j in range(8):
                t = op("vector", lambda e, j=j: e.bn_aggr(mv[:, j, :], stats[:, j, :]), t, *st["ln"])
            t = op("vector", lambda e: e.tensor_scalar(rs[:, :], mv[:, :, 1], eps, None, ALU.add), t)
            t = op("gpsimd", lambda e: e.tensor_tensor(rs[:, :], rs[:, :], mhalf, ALU.pow), t)
            t = op("vector", lambda e: e.scalar_tensor_tensor(
                nm[:, :], mv[:, :, 0], -1.0, rs[:, :], ALU.mult, ALU.mult), t)
            w = [op("scalar", lambda e, j=j: e.activation(
                dst(j), src(j), ACT.Identity, bias=nm[:, j:j + 1], scale=rs[:, j:j + 1]), t)
                for j in range(8)]
            st["ln"] = (w[-1],)
            return w

        def transposed(src, dst, after, free, w):
            for h in range(2):
                w.append([])
                for c in range(2):
                    i, ps, fr = gen.take()
                    for j in range(4):
                        t = op("tensor", lambda e, j=j, c=c, h=h, ps=ps: e.transpose(
                            ps[:, 128 * j:128 * j + 128], src(4 * h + j)[:, 128 * c:128 * c + 128],
                            ident), t_c, after[4 * h + j], *fr)
                    t = op("scalar", lambda e, c=c, h=h, ps=ps: e.copy(
                        dst[:, c, 512 * h:512 * h + 512], ps[:, :]), t, *free)
                    gen.give(i, t)
                    w[h].append(t)
                    yield

        def prep(b):
            p = b % 2
            r = R[b] = {}
            w = layernorm(lambda j: xnb[:, j, :], lambda j: xnb[:, j, :],
                          *[(x_t[b, j // 2], t_c) for j in range(8)])
            yield
            xt = []
            yield from transposed(lambda j: xnb[:, j, :], xnT, w, st["TB"], xt)
            a = [op("gpsimd", lambda e: e.memset(xcp[:, :, 0:1], 0.0), xt[1][1]),
                 op("gpsimd", lambda e: e.memset(xcp[:, :, 1025:1026], 0.0), xt[1][1])]
            cv, txs = [], []
            for c in range(2):
                for h in range(2):
                    i, ps, fr = gen.take()
                    for k in range(2):
                        t = op("tensor", lambda e, c=c, h=h, k=k, ps=ps: e.matmul(
                            ps[:, :], wxz[:, k, 128 * c:128 * c + 128],
                            xnT[:, k, 512 * h:512 * h + 512], start=k == 0, stop=k == 1), *xt[h], *fr)
                    t = op("scalar", lambda e, c=c, h=h, ps=ps: e.copy(
                        xcp[:, c, 1 + 512 * h:513 + 512 * h], ps[:, :]), t, xt[1][1])
                    gen.give(i, t)
                    a.append(t)
                    yield
                t = op("vector", lambda e, c=c: e.tensor_scalar(
                    xs[p][:, c, :], xcp[:, c, 1:1025], cw[:, c, 1:2], None, ALU.mult), *a, *st.get(f"xs{p}", ()))
                t = op("vector", lambda e, c=c: e.scalar_tensor_tensor(
                    xs[p][:, c, :], xcp[:, c, 0:1024], cw[:, c, 0:1], xs[p][:, c, :], ALU.mult, ALU.add), t)
                t = op("vector", lambda e, c=c: e.scalar_tensor_tensor(
                    xs[p][:, c, :], xcp[:, c, 2:1026], cw[:, c, 2:3], xs[p][:, c, :], ALU.mult, ALU.add), t)
                cv.append(t)
            yield
            for c in range(2):
                txs.append(op("scalar", lambda e, c=c: e.activation(
                    xs[p][:, c, :], xs[p][:, c, :], ACT.Silu), cv[c]))
            r["xs"] = txs[1]
            for g in range(4):
                i, ps, fr = gen.take()
                for j in range(2):
                    for k in range(2):
                        t = op("tensor", lambda e, g=g, j=j, k=k, ps=ps: e.matmul(
                            ps[:, 256 * j:256 * j + 256], xnT[:, k, 128 * (2 * g + j):128 * (2 * g + j) + 128],
                            wxz[:, k, 256:512], start=k == 0, stop=k == 1), *xt[1], *fr)
                z = op("scalar", lambda e, g=g, ps=ps: e.activation(
                    zsl[p][:, 2 * g:2 * g + 2, :], ps[:, :], ACT.Silu), t, *st.get(f"zs{p}", ()))
                gen.give(i, z)
                yield
            r["zs"] = z
            st["TB"] = (t,)
            tdc, tb = [], []
            for h in range(2):
                sl = slice(512 * h, 512 * h + 512)
                i, ps, fr = gen.take()
                for k in range(2):
                    t = op("tensor", lambda e, sl=sl, k=k, ps=ps: e.matmul(
                        ps[0:80, :], wx[:, k, 0:80], xs[p][:, k, sl],
                        start=k == 0, stop=k == 1), *txs, t_wx, *fr)
                t = op("scalar", lambda e, sl=sl, ps=ps: e.copy(
                    dcb[p][0:80, sl], ps[0:80, :]), t, *st.get(f"dc{p}", ()))
                tdc.append(t)
                gen.give(i, t)
                yield
            r["dc"] = tdc[1]
            v, m = [], []
            for h in range(2):
                sl = slice(512 * h, 512 * h + 512)
                for c in range(2):
                    i, ps, fr = gen.take()
                    t = op("tensor", lambda e, c=c, sl=sl, ps=ps: e.matmul(
                        ps[:, :], wdc[0:64, 128 * c:128 * c + 128], dcb[p][0:64, sl],
                        start=True, stop=True), tdc[h], t_v, *fr)
                    u = op("scalar", lambda e, c=c, sl=sl, ps=ps: e.activation(
                        dts[p][:, c, sl], ps[:, :], ACT.Relu, bias=bdt[:, c:c + 1]),
                        t, *st.get(f"dt{p}", ()))
                    a = op("scalar", lambda e, c=c, sl=sl, ps=ps: e.activation(
                        spt[:, c, sl], ps[:, :], ACT.Abs, bias=bdt[:, c:c + 1]), t, *st["TB"])
                    gen.give(i, u, a)
                    v.append(a)
                    m.append(u)
                yield
            for c in range(2):
                t = op("scalar", lambda e, c=c: e.activation(
                    spt[:, c, :], spt[:, c, :], ACT.Exp, scale=-1.0), *v)
            for h in range(2):
                sl = slice(512 * h, 512 * h + 512)
                i, ps, fr = gen.take()
                for k in range(2):
                    tm = op("tensor", lambda e, sl=sl, k=k, ps=ps: e.matmul(
                        ps[0:96, :], wx[:, k, 80:176], xs[p][:, k, sl],
                        start=k == 0, stop=k == 1), *fr)
                tm = op("scalar", lambda e, sl=sl, ps=ps: e.copy(btmp[0][:, sl], ps[0:96, :]), tm, *cv)
                gen.give(i, tm)
                tb.append(tm)
                yield
            lnw = []
            for c in range(2):
                lnw.append(op("scalar", lambda e, c=c: e.activation(
                    spt[:, c, :], spt[:, c, :], ACT.Ln, bias=1.0), t))
            td = []
            for c in range(2):
                td.append(op("vector", lambda e, c=c: e.scalar_tensor_tensor(
                    dts[p][:, c, :], spt[:, c, :], 1e-5, dts[p][:, c, :], ALU.add, ALU.add), lnw[c], *m))
            r["dt"] = td[1]
            st["TB"] = (td[1],)
            ue = "vector" if b == 0 else "gpsimd"
            for c in range(2):
                t = op(ue, lambda e, c=c: e.tensor_tensor(
                    us[p][:, c, :], dts[p][:, c, :], xs[p][:, c, :], ALU.mult), td[c], r["xs"], *st.get(f"u{p}", ()))
            r["u"] = t
            yield
            t = op("vector", lambda e: e.tensor_copy(bst[p][0:96, :], btmp[0]), *tb, *st.get(f"bst{p}", ()))
            t = op("vector", lambda e: e.tensor_tensor(btmp[1], btmp[0], bst[p][0:96, :], ALU.subtract), t)
            t1 = op("vector", lambda e: e.tensor_copy(bst[p][0:64, :], btmp[1][0:64, :]), t)
            t = op("vector", lambda e: e.tensor_tensor(
                btmp[0][0:32, :], btmp[1][0:32, :], bst[p][0:32, :], ALU.subtract), t1)
            r["bst"] = op("vector", lambda e: e.tensor_copy(bst[p][0:32, :], btmp[0][0:32, :]), t)
            st["TA"] = (r["bst"],)
            if b + 1 < NB:
                load_x(b + 1)
            yield

        GROUP = 4

        def main(b):
            p, r = b % 2, R[b]
            nxt = {}

            def spread(k):
                i, bb, fr = bbr.take()
                for h in range(2):
                    n = k % 16
                    t = op("tensor", lambda e, h=h, bb=bb, n=n: e.matmul(
                        bb[h][:, :], SEL[:, n:n + 1].to_broadcast([96, 128]),
                        bst[p][0:96, 512 * h:512 * h + 512], start=True, stop=True), r["bst"], t_v, *fr)
                nxt[k] = (i, bb, t)

            spread(0)
            wait = []
            for c in range(2):
                free = st.get("ssum", ())

                def add(S, n, is_, t):
                    for h in range(2):
                        t2 = op("tensor", lambda e, h=h: e.matmul(
                            ssum[h][:, :], ident, S[:, 512 * h:512 * h + 512],
                            start=n == GROUP - 1, stop=n == 15), t, *free)
                    ringS.give(is_, t2)
                    return t2

                for n in range(16):
                    k = 16 * c + n
                    if k < 31:
                        spread(k + 1)
                    ia, A, fa = ringA.take()
                    t_a = op("scalar", lambda e, A=A, c=c, n=n: e.activation(
                        A, dts[p][:, c, :], ACT.Exp, scale=nea[:, c, n:n + 1]), r["dt"], t_nea, *fa)
                    i, bb, t_b = nxt[k]
                    ib, Bx, fb = ringB.take()
                    for h in range(2):
                        t = op("vector", lambda e, h=h, bb=bb, Bx=Bx, c=c: e.tensor_tensor(
                            Bx[:, 512 * h:512 * h + 512], us[p][:, c, 512 * h:512 * h + 512],
                            bb[h][:, :], ALU.mult), t_b, r["u"], *fb)
                    bbr.give(i, t)
                    is_, S, fs = ringS.take()
                    t_sc = op("vector", lambda e, A=A, Bx=Bx, S=S: e.tensor_tensor_scan(
                        S, A, Bx, 0.0, ALU.mult, ALU.add), t_a, t, *fs)
                    ringA.give(ia, t_sc)
                    ringB.give(ib, t_sc)
                    if wait:
                        t_sum = add(*wait.pop())
                    if n % GROUP == 0:
                        S0, i0, t_p = S, is_, t_sc
                    else:
                        t_p = op("gpsimd", lambda e, S=S, S0=S0: e.tensor_tensor(S0, S0, S, ALU.add), t_p, t_sc)
                        ringS.give(is_, t_p)
                    if n % GROUP == GROUP - 1:
                        wait.append((S0, n, i0, t_p))
                    if n == 4:
                        for h in range(2):
                            i2, ps, fr = gen.take()
                            sl = slice(512 * h, 512 * h + 512)
                            t = op("tensor", lambda e, c=c, sl=sl, ps=ps: e.matmul(
                                ps[:, :], wdc[64:80, 128 * c:128 * c + 128], dcb[p][64:80, sl],
                                start=True, stop=True), r["dc"], *fr)
                            t_cs = op("scalar", lambda e, sl=sl, ps=ps: e.copy(
                                Cs[:, sl], ps[:, :]), t, *st["Cs"])
                            gen.give(i2, t_cs)
                            st[f"dc{p}"] = (t,)
                    if n < 15:
                        yield
                t_sum = add(*wait.pop())
                for h in range(2):
                    sl = slice(512 * h, 512 * h + 512)
                    t = op("vector", lambda e, sl=sl, c=c, h=h: e.tensor_tensor(
                        yb[:, c, sl], Cs[:, sl], ssum[h][:, :], ALU.mult), t_sum, t_cs, *st["PA"])
                st["ssum"] = (t,)
                st["Cs"] = (t,)
                t = op("vector", lambda e, c=c: e.scalar_tensor_tensor(
                    yb[:, c, :], xs[p][:, c, :], Dp[:, c:c + 1], yb[:, c, :], ALU.mult, ALU.add), t, r["xs"])
                if c == 1:
                    r["y"] = t
                    st[f"xs{p}"] = (t, r["u"])
                    st[f"dt{p}"] = (t_a, r["u"])
                    st[f"u{p}"] = (t_sc,)
                    st[f"bst{p}"] = (t_b,)
                yield

        def post(b):
            p, r = b % 2, R[b]
            t_x = dma("sync", lane("X"), lambda e: e.dma_start(X, rows8(x[b])), *st["X"])
            gt = []
            for g in range(4):
                i, ps, fr = gen.take()
                for j in range(2):
                    for k in range(2):
                        t = op("tensor", lambda e, g=g, j=j, k=k, ps=ps: e.matmul(
                            ps[:, 256 * j:256 * j + 256], yb[:, k, 128 * (2 * g + j):128 * (2 * g + j) + 128],
                            wout[:, k, :], start=k == 0, stop=k == 1), r["y"], *fr)
                st["PA"] = (t,)
                t = op("vector", lambda e, g=g, ps=ps: e.tensor_tensor(
                    gb[:, 2 * g:2 * g + 2, :], zsl[p][:, 2 * g:2 * g + 2, :],
                    ps[:, :].rearrange("p (j d) -> p j d", j=2), ALU.mult), t, r["zs"], *st["PB"])
                gen.give(i, t)
                gt += [t, t]
                yield
            st[f"zs{p}"] = (t,)
            w = layernorm(lambda j: gb[:, j, :], lambda j: gb[:, j, :], *[(t,) for t in gt])
            yield
            ta = []
            for h in range(4):
                sl = slice(2 * h, 2 * h + 2)
                ta.append(op("gpsimd", lambda e, sl=sl: e.tensor_tensor(
                    X[:, sl, :], X[:, sl, :], gb[:, sl, :], ALU.add), w[2 * h + 1], t_x))
            o1 = dma("sync", lane("x1"), lambda e: e.dma_start(
                rows8(x1_d[TB * b:TB * (b + 1), :]), X), ta[3])
            yield
            w = layernorm(lambda j: X[:, j, :], lambda j: gb[:, j, :], *[(ta[j // 2],) for j in range(8)])
            o2 = dma("sync", lane("xn"), lambda e: e.dma_start(
                rows8(xn_d[TB * b:TB * (b + 1), :]), gb), w[7])
            r["stored"] = (o1, o2)
            st["X"] = (o1, w[7])
            yield
            xt = []
            yield from transposed(lambda j: gb[:, j, :], nT, w, st["nT"], xt)
            r["nT"] = xt
            st["PB"] = (o2, xt[1][1])
            i, ps, fr = gen.take()
            for j in range(8):
                for k in range(2):
                    t = op("tensor", lambda e, j=j, k=k, ps=ps: e.matmul(
                        ps[:, 8 * j:8 * j + 8], nT[:, k, 128 * j:128 * j + 128], wg[:, k, :],
                        start=k == 0, stop=k == 1), *xt[j // 4], *fr)
            t = op("scalar", lambda e, ps=ps: e.copy(
                lg[:, 8 * b:8 * b + 8, :], ps[:, 0:64].rearrange("p (j e) -> p j e", j=8)), t)
            gen.give(i, t)
            r["lg"] = t
            yield

        def shared(b):
            r = R[b]
            for g in range(4):
                xt = r["nT"][g // 2]
                hw = []
                for f in range(0, 8, 2):
                    i, ps, fr = gen.take()
                    for a in range(2):
                        for k in range(2):
                            t = op("tensor", lambda e, f=f + a, a=a, k=k, g=g, ps=ps: e.matmul(
                                ps[:, 256 * a:256 * a + 256], s1[:, k, 128 * f:128 * f + 128],
                                nT[:, k, 256 * g:256 * g + 256], start=k == 0, stop=k == 1), t_s, *xt, *fr)
                    st["nT"] = (t,)
                    for a in range(2):
                        t = op("scalar", lambda e, f=f + a, a=a, ps=ps: e.activation(
                            hT[:, f, :], ps[:, 256 * a:256 * a + 256], ACT.Gelu, bias=sb1t[:, f:f + 1]),
                            t, *st["hT"])
                        hw.append(t)
                    gen.give(i, t)
                    yield
                i, ps, fr = gen.take()
                for j in range(2):
                    for f in range(8):
                        t = op("tensor", lambda e, j=j, f=f, ps=ps: e.matmul(
                            ps[:, 256 * j:256 * j + 256], hT[:, f, 128 * j:128 * j + 128], s2[:, f, :],
                            start=f == 0, stop=f == 7), hw[f], *fr)
                        if (f, j) in ((3, 0), (7, 0), (3, 1)):
                            yield
                st["hT"] = (t,)
                io, O, fo = ringO.take()
                for j in range(2):
                    t2 = op("vector", lambda e, j=j, ps=ps, O=O: e.tensor_tensor(
                        O[:, j, :], sb2t[:, :], ps[:, 256 * j:256 * j + 256], ALU.add), t, t_s, *fo)
                gen.give(i, t2)
                o = dma("sync", lane(f"sh{io}"), lambda e, g=g, O=O: e.dma_start(
                    rows8(sh_d[TB * b + 256 * g:TB * b + 256 * g + 256, :]), O), t2)
                ringO.give(io, o)
                r.setdefault("sh", []).append(o)
                yield

        def chain(*gens):
            for g in gens:
                yield from g

        def weave(front, steps, side, total):
            done = 0
            for s, _ in enumerate(front):
                while done * steps < total * (s + 1):
                    done += 1
                    next(side, None)
            for _ in side:
                pass

        NPREP, NPOST, NSH = 22, 12, 32
        for _ in prep(0):
            pass
        for b in range(NB):
            side, total = [], 0
            if b:
                side += [post(b - 1), shared(b - 1)]
                total += NPOST + NSH
            if b + 1 < NB:
                side.append(prep(b + 1))
                total += NPREP
            weave(main(b), 32, chain(*side), total)
        for _ in post(NB - 1):
            pass
        last = [(q.sems[e], q.count[e], e) for e in q.ENGINES if q.count[e]]
        for b in range(NB):
            last += list(R[b]["stored"])

        fill = shared(NB - 1)

        def filler(n):
            for _ in range(n):
                next(fill, None)

        at[0] = kept
        oh_at = at[0]
        OHp = cut(2 * 4096).rearrange("p (n m) -> p n m", m=128)
        OHq = cut(2 * 32 * NCOL).rearrange("p (n m) -> p n m", m=NCOL)
        rb = cut(256 * 12)
        at3 = [0]

        def r3(n=256):
            at3[0] += n
            return rb[:, at3[0] - n:at3[0]]

        def v3(a):
            return a.rearrange("p (j e) -> p j e", e=8)

        def over_e(a):
            return a.unsqueeze(2).to_broadcast([128, NTOK, 8])

        def over_j(a):
            return a.unsqueeze(1).to_broadcast([128, NTOK, 8])

        pr, oh1, oh2, eq, M, pre, tot, inc = (r3() for _ in range(8))
        mx, z, ix, m1, m2, cnt = (r3(32) for _ in range(6))
        nt, ts, te, bs = (r3(8) for _ in range(4))
        ntb = r3(128)
        te8 = cut(NTILE * 8)
        texf = cut(NTILE)
        posi, qi, pi = (cut(64).bitcast(i32) for _ in range(3))
        posf, qf, pf = cut(64), cut(64), cut(64)
        vt, ve, vi = cut(NCOL), cut(NCOL), cut(NCOL).bitcast(i32)

        def dve(fn, *after):
            return op("vector", fn, *after)

        t = dve(lambda e: e.reduce_max(mx, lg[:, :, :], axis=AX.X), *last)
        t = dve(lambda e: e.tensor_tensor(v3(pr), lg[:, :, :], over_e(mx), ALU.subtract), t)
        t = op("scalar", lambda e: e.activation(pr, pr, ACT.Exp), t)
        t = dve(lambda e: e.reduce_sum(z, v3(pr), axis=AX.X), t)
        t = dve(lambda e: e.reciprocal(z, z), t)
        t = dve(lambda e: e.tensor_tensor(v3(pr), v3(pr), over_e(z), ALU.mult), t)

        def best(oh, m, t):
            t = dve(lambda e: e.reduce_max(m, v3(pr), axis=AX.X), t)
            t = dve(lambda e: e.tensor_tensor(v3(eq), v3(pr), over_e(m), ALU.is_equal), t)
            t = dve(lambda e: e.tensor_tensor(v3(eq), v3(eq), over_j(iom8), ALU.mult), t)
            t = dve(lambda e: e.tensor_reduce(ix, v3(eq), axis=AX.X, op=ALU.min), t)
            return dve(lambda e: e.tensor_tensor(v3(oh), over_e(ix), over_j(iom8), ALU.is_equal), t)

        t = best(oh1, m1, t)
        t = dve(lambda e: e.scalar_tensor_tensor(pr, oh1, -2.0, pr, ALU.mult, ALU.add), t)
        t = best(oh2, m2, t)
        t_m = dve(lambda e: e.tensor_tensor(M, oh1, oh2, ALU.add), t)
        filler(5)
        op("tensor", lambda e: e.matmul(PS[0][:, 0:256], tri, M, start=True, stop=True), t_m, *last)
        t = op("tensor", lambda e: e.matmul(PS[1][:, 0:256], ones, M, start=True, stop=True), t_m)
        t = dve(lambda e: e.tensor_copy(tot, PS[1][:, 0:256]), t)
        dve(lambda e: e.tensor_copy(pre, PS[0][:, 0:256]))
        for x8 in range(8):
            t2 = dve(lambda e, x8=x8: e.tensor_tensor_scan(
                v3(inc)[:, :, x8], ones[:, 0:NTOK], v3(tot)[:, :, x8], 0.0, ALU.mult, ALU.add), t)
        t = dve(lambda e: e.tensor_copy(cnt[:, 0:8], v3(inc)[:, NTOK - 1, :]), t2)
        nt3 = ntb.rearrange("p (e i) -> p e i", i=16)
        t = dve(lambda e: e.tensor_tensor(nt3, cnt[:, 0:8].unsqueeze(2).to_broadcast([128, 8, 16]),
                                          thr.unsqueeze(1).to_broadcast([128, 8, 16]), ALU.is_gt), t)
        t = dve(lambda e: e.reduce_sum(nt, nt3, axis=AX.X), t)
        t_te = dve(lambda e: e.tensor_tensor_scan(te, ones[:, 0:8], nt, 0.0, ALU.mult, ALU.add), t)
        te3 = te8.rearrange("p (i e) -> p i e", e=8)
        t8 = dve(lambda e: e.tensor_tensor(te3, tidx.unsqueeze(2).to_broadcast([128, NTILE, 8]),
                                           te.unsqueeze(1).to_broadcast([128, NTILE, 8]), ALU.is_ge), t_te)
        t = dve(lambda e: e.tensor_tensor(ts, te, nt, ALU.subtract), t_te)
        t8 = dve(lambda e: e.reduce_sum(texf, te3, axis=AX.X), t8)
        t = dve(lambda e: e.tensor_scalar(bs, ts, float(ROWS), None, ALU.mult), t)
        t_ex = dve(lambda e: e.tensor_scalar(texp[:, :], texf, 7.0, None, ALU.min), t8)
        t2 = dve(lambda e: e.tensor_tensor(pre, pre, inc, ALU.add), t2)
        t2 = dve(lambda e: e.tensor_tensor(pre, pre, tot, ALU.subtract), t2)
        t = dve(lambda e: e.tensor_tensor(v3(pre), v3(pre), over_j(bs), ALU.add), t, t2)
        for k, oh in enumerate((oh1, oh2)):
            t1 = dve(lambda e, oh=oh: e.tensor_tensor(oh, oh, pre, ALU.mult), t)
            t1 = dve(lambda e, k=k, oh=oh: e.reduce_sum(posf[:, 32 * k:32 * k + 32], v3(oh), axis=AX.X), t1)
        t = dve(lambda e: e.tensor_copy(posi, posf), t1)
        tq = dve(lambda e: e.tensor_scalar(qi, posi, 7, None, ALU.logical_shift_right), t)
        tp = dve(lambda e: e.tensor_scalar(pi, posi, 127, None, ALU.bitwise_and), t)
        tq = dve(lambda e: e.tensor_copy(qf, qi), tq)
        tp = dve(lambda e: e.tensor_copy(pf, pi), tp)
        filler(15)
        TAB = PS[2][:, 0:NCOL]
        for h in range(4):
            sl = slice(16 * h, 16 * h + 16)
            t = dve(lambda e, sl=sl: e.tensor_tensor(
                OHq[:, sl, :], qf[:, sl].unsqueeze(2).to_broadcast([128, 16, NCOL]),
                i128[:, 0:NCOL].unsqueeze(1).to_broadcast([128, 16, NCOL]), ALU.is_equal), tq)
            t1 = dve(lambda e, sl=sl: e.tensor_tensor(
                OHp[:, sl, :], pf[:, sl].unsqueeze(2).to_broadcast([128, 16, 128]),
                i128.unsqueeze(1).to_broadcast([128, 16, 128]), ALU.is_equal), tp)
            t = dve(lambda e, sl=sl: e.tensor_tensor(
                OHq[:, sl, :], OHq[:, sl, :], vtok[:, sl].unsqueeze(2).to_broadcast([128, 16, NCOL]), ALU.mult), t)
            for n in range(16 * h, 16 * h + 16):
                t2 = op("tensor", lambda e, n=n: e.matmul(
                    TAB, OHp[:, n, :], OHq[:, n, :], start=n == 0, stop=n == 63), t, t1)
            if h < 3:
                filler(3)
        for _ in fill:
            pass
        t = dve(lambda e: e.tensor_scalar(vt, TAB, float(2 * T), None, ALU.add), t2)
        t_v2 = dve(lambda e: e.tensor_copy(ids[:, :], vt), t)
        t_idg = dve(lambda e: e.tensor_scalar(idg[:, :], ids[:, :], T - 1, None, ALU.bitwise_and), t_v2)
        t = dve(lambda e: e.tensor_tensor(z, m1, m2, ALU.add))
        t = dve(lambda e: e.reciprocal(z, z), t)
        dve(lambda e: e.tensor_tensor(wts[:, 0, :], m1, z, ALU.mult), t)
        t_w = dve(lambda e: e.tensor_tensor(wts[:, 1, :], m2, z, ALU.mult), t)

        w1v = W1.rearrange("e (c p) f -> e p c f", p=128)
        w2v = W2.rearrange("e (c p) h -> e p c h", p=128)
        NW = 2
        ringW = Ring([(cut(2048).rearrange("p (c f) -> p c f", c=2),
                       cut(2048).rearrange("p (c h) -> p c h", c=8), cut(8), cut(256)) for _ in range(NW)])
        ringG = Ring([cut(512).rearrange("p (j d) -> p j d", j=2) for _ in range(3)])
        ringX = Ring([cut(512).rearrange("p (c t) -> p c t", c=2) for _ in range(2)])
        ringH = Ring([cut(2048).rearrange("p (f t) -> p f t", f=8) for _ in range(2)])
        ringY = Ring([cut(512).rearrange("p (j d) -> p j d", j=2) for _ in range(3)])
        pX, pH, pY = Ring(PS[0:2]), Ring(PS[3:6]), Ring(PS[6:8])
        done = [(q.sems[e], q.count[e], e) for e in ("tensor", "scalar", "vector")]
        regs = {}

        def read(i):
            def fn(e):
                regs[i] = e.value_load(texp[0:1, i:i + 1], min_val=0, max_val=E - 1)
                return e.dma_start(Ws[i][1][0], w1v[bass.ds(regs[i], 1)].squeeze(0))
            return fn

        def part(i, n, src):
            return lambda e: e.dma_start(Ws[i][1][n], src(regs[i]))

        Ws, G, XT = {}, {}, {}

        def weights(i):
            iw, W, fw = ringW.take()
            Ws[i] = (iw, W)
            ln = lane(f"W{iw}")
            dma("sync", ln, read(i), t_ex, *fw, *last)
            dma("sync", ln, part(i, 1, lambda v: w2v[bass.ds(v, 1)].squeeze(0)))
            dma("sync", ln, part(i, 2, lambda v: b1[bass.ds(v, 1)].squeeze(0)))
            Ws[i] += (dma("sync", ln, part(i, 3, lambda v: b2[bass.ds(v, 1)].to_broadcast([128, D]))),)

        def gather(i):
            ig, g, fg = ringG.take()
            for j in range(2):
                t = dma("gpsimd", lane(f"G{ig}"), lambda e, g=g, j=j: e.indirect_dma_start(
                    g[:, j, :], None, xn_d,
                    bass.IndirectOffsetOnAxis(ap=idg[:, 2 * i + j:2 * i + j + 1].bitcast(u32), axis=0)),
                    t_idg, *fg, *last)
            G[i] = (ig, g, t)

        def turn(i):
            ig, g, t_g = G[i]
            ix_, ps, fr = pX.take()
            for c in range(2):
                for j in range(2):
                    t = op("tensor", lambda e, c=c, j=j, ps=ps, g=g: e.transpose(
                        ps[:, 256 * c + 128 * j:256 * c + 128 * j + 128], g[:, j, 128 * c:128 * c + 128],
                        ident), t_g, *done, *fr)
            ringG.give(ig, t)
            ixs, xT, fx = ringX.take()
            t_x = op("vector", lambda e, ps=ps, xT=xT: e.tensor_copy(
                xT, ps[:, :].rearrange("p (c t) -> p c t", c=2)), t, *fx)
            pX.give(ix_, t_x)
            XT[i] = (ixs, xT, t_x)

        for i in range(min(NW, NTILE)):
            weights(i)
        for i in range(3):
            gather(i)
        turn(0)
        scat = []
        for i in range(NTILE):
            iw, (w1, w2, bb1, bb2), t_wt = Ws[i]
            ixs, xT, t_x = XT[i]
            ih, h, fh = ringH.take()
            hw = []
            for f in range(0, 8, 2):
                ip, ps, fr = pH.take()
                for a in range(2):
                    for k in range(2):
                        t = op("tensor", lambda e, f=f + a, a=a, k=k, ps=ps, w1=w1, xT=xT: e.matmul(
                            ps[:, 256 * a:256 * a + 256], w1[:, k, 128 * f:128 * f + 128], xT[:, k, :],
                            start=k == 0, stop=k == 1), t_x, t_wt, *fr)
                for a in range(2):
                    t2 = op("scalar", lambda e, f=f + a, a=a, ps=ps, h=h, bb1=bb1: e.activation(
                        h[:, f, :], ps[:, 256 * a:256 * a + 256], ACT.Gelu, bias=bb1[:, f:f + 1]), t, t_wt, *fh)
                    hw.append(t2)
                pH.give(ip, t2)
            ringX.give(ixs, t)
            if i + 1 < NTILE:
                turn(i + 1)
            ip, ps, fr = pY.take()
            for j in range(2):
                for f in range(8):
                    t = op("tensor", lambda e, j=j, f=f, ps=ps, h=h, w2=w2: e.matmul(
                        ps[:, 256 * j:256 * j + 256], h[:, f, 128 * j:128 * j + 128], w2[:, f, :],
                        start=f == 0, stop=f == 7), hw[f], *fr)
            ringH.give(ih, t)
            iy, y, fy = ringY.take()
            for j in range(2):
                t2 = op("vector", lambda e, j=j, ps=ps, y=y, bb2=bb2: e.tensor_tensor(
                    y[:, j, :], bb2, ps[:, 256 * j:256 * j + 256], ALU.add), t, t_wt, *fy)
            pY.give(ip, t2)
            ringW.give(iw, t2, t)
            if i + 3 < NTILE:
                gather(i + 3)
            for j in range(2):
                o = dma("gpsimd", lane(f"Y{iy}"), lambda e, i=i, j=j, y=y: e.indirect_dma_start(
                    z_d, bass.IndirectOffsetOnAxis(ap=ids[:, 2 * i + j:2 * i + j + 1].bitcast(u32), axis=0),
                    y[:, j, :], None, bounds_check=2 * T - 1, oob_is_err=False), t2, t_v2)
            ringY.give(iy, o)
            scat = (scat + [o])[-3:]
            if i + NW < NTILE:
                weights(i + NW)

        top = at[0]
        at[0] = oh_at
        ringL = Ring([tuple(cut(2048).rearrange("p (j d) -> p j d", j=8) for _ in range(2)) for _ in range(3)])
        assert at[0] <= oh_at + 2 * 4096 + 2 * 32 * NCOL
        at[0] = top
        ringZ = Ring([tuple(cut(512).rearrange("p (j d) -> p j d", j=2) for _ in range(2)) for _ in range(4)])
        Lb = {}
        for b in range(NB):
            if b < 3:
                Lb[b] = ringL.take()

        def load_l(b):
            il, (XX, S), fl = Lb[b]
            rows = slice(TB * b, TB * (b + 1))
            dma("sync", lane(f"L{il}"), lambda e, rows=rows, S=S: e.dma_start(
                S, rows8(sh_d[rows, :])), *done, *R[b]["sh"], *fl)
            Lb[b] += (dma("sync", lane(f"L{il}"), lambda e, rows=rows, XX=XX: e.dma_start(
                XX, rows8(x1_d[rows, :])), *R[b]["stored"], *fl),)
        for b in range(3):
            load_l(b)
        for b in range(NB):
            if b == 3:
                Lb[b] = ringL.take()
                load_l(b)
            il, (XX, S), fl, t_l = Lb[b]
            sw = []
            for g in range(4):
                iz, Z, fz = ringZ.take()
                for k in range(2):
                    r0 = T * k + TB * b + 256 * g
                    t_z = dma("scalar" if k else "sync", lane(f"Z{iz}"), lambda e, k=k, Z=Z, r0=r0: e.dma_start(
                        Z[k], rows8(z_d[r0:r0 + 256, :])), *scat, *last, *fz)
                for j in range(2 * g, 2 * g + 2):
                    n = 8 * b + j
                    for k in range(2):
                        t = dve(lambda e, j=j, n=n, k=k, S=S, Z=Z: e.scalar_tensor_tensor(
                            S[:, j, :], Z[k][:, j % 2, :], wts[:, k, n:n + 1], S[:, j, :], ALU.mult, ALU.add),
                            t_z, t_l, t_w, *([t] if k else []))
                    sw.append((t,))
                ringZ.give(iz, t)
            w = layernorm(lambda j, S=S: S[:, j, :], lambda j, S=S: S[:, j, :], *sw)
            outs = []
            for h in range(2):
                sl = slice(4 * h, 4 * h + 4)
                t = dve(lambda e, XX=XX, S=S, sl=sl: e.tensor_tensor(
                    XX[:, sl, :], XX[:, sl, :], S[:, sl, :], ALU.add), w[4 * h + 3], t_l)
                outs.append(dma("sync", lane(f"out{h}"), lambda e, b=b, XX=XX, sl=sl: e.dma_start(
                    rows8(out[b])[:, sl, :], XX[:, sl, :]), t))
            ringL.give(il, *outs)

        block = ctx.enter_context(nc.Block())

        @block.tensor
        def _(eng):
            q.play("tensor", eng)

        @block.vector
        def _(eng):
            q.play("vector", eng)

        @block.scalar
        def _(eng):
            q.play("scalar", eng)

        @block.gpsimd
        def _(eng):
            q.play("gpsimd", eng)

        @block.sync
        def _(eng):
            q.play("sync", eng)
            for ln in lanes.values():
                eng.wait_ge(ln.sem, ln.count)


def kernel(**inputs):
    import numpy as np
    import concourse.bacc as bacc
    from concourse import mybir as mb
    from concourse.bass_utils import run_bass_kernel_spmd as run
    import ml_dtypes

    def a(name):
        return np.ascontiguousarray(inputs[name])

    def t(name):
        return np.ascontiguousarray(np.asarray(inputs[name]).T)

    def cols(name):
        return np.ascontiguousarray(np.asarray(inputs[name]).reshape(-1, 128).T)

    cst = np.zeros((128, CW), np.float32)
    cst[:, CI:CI + 128] = np.eye(128)
    cst[:, CT:CT + 128] = np.triu(np.ones((128, 128)), 1)
    cst[:, CO:CO + 128] = 1.0
    cst[:, CM8:CM8 + 8] = np.arange(8) - 8.0
    cst[:, CTH:CTH + 16] = np.arange(16) * float(ROWS)
    cst[:, CTI:CTI + NTILE] = np.arange(NTILE)
    cst[:, CMH:CMH + 8] = -0.5
    cst[:, CEP] = 1e-5
    cst[:, CP] = np.arange(128)
    cst[:, CR:CR + 128] = np.arange(128)
    cst[:, CV:CV + 64] = np.arange(64) * 128.0 + np.arange(128)[:, None] - 2.0 * T
    sel = np.zeros((96, 16), ml_dtypes.bfloat16)
    for g in range(3):
        sel[32 * g:32 * g + 16] = np.eye(16)
    A, Fp = "L0_attn_", "L0_ffn_"
    arrays = {
        "x": a(A + "x"), "W_inT": t(A + "W_in"), "conv_w": a(A + "conv_w"), "W_xT": t(A + "W_x"),
        "W_dtT": t(A + "W_dt"), "b_dt": cols("L0_attn_b_dt"), "A_log": a(A + "A_log"), "D_param": cols("L0_attn_D_param"),
        "W_CT": t(A + "W_C"), "W_outT": t(A + "W_out"), "gate_wT": t(Fp + "gate_w"),
        "W1": a(Fp + "W1"),
        "b1": np.ascontiguousarray(np.asarray(inputs[Fp + "b1"]).reshape(E, 8, 128).transpose(0, 2, 1)),
        "W2": a(Fp + "W2"), "b2": a(Fp + "b2"), "sW1": a(Fp + "sW1"),
        "sb1": cols("L0_ffn_sb1"),
        "sW2": a(Fp + "sW2"), "sb2": a(Fp + "sb2"),
        "cst": cst, "sel": sel,
    }
    nc = bacc.Bacc("TRN2", target_bir_lowering=False, num_devices=1)
    aps = {n: nc.dram_tensor(n, v.shape, mb.dt.from_np(v.dtype), kind="ExternalInput").ap()
           for n, v in arrays.items()}
    out = nc.dram_tensor("out", (NB, TB, D), mb.dt.float32, kind="ExternalOutput").ap()
    build(nc, out=out, **aps)
    r = run(nc, [arrays], core_ids=[0])
    return r.results[0]["out"]
```

```python
import concourse.bass as bass
from concourse import mybir
from contextlib import ExitStack

T, D, F, E, NB, TB = 4096, 256, 1024, 8, 4, 1024
NTOK = T // 128
ROWS = 256
NTILE = (2 * T + E * (ROWS - 1)) // ROWS
NCOL = NTILE * ROWS // 128
CI, CT, CO, CM8, CTH, CTI, CMH, CEP, CP, CR, CV = 0, 128, 256, 384, 392, 408, 448, 456, 457, 458, 586
CW = 650


class Queues:

    ENGINES = ("tensor", "vector", "scalar", "gpsimd", "sync")

    def __init__(self, sem):
        self.items = {e: [] for e in self.ENGINES}
        self.sems = {e: sem("s_" + e) for e in self.ENGINES}
        self.count = {e: 0 for e in self.ENGINES}

    def op(self, engine, fn, *after):
        self.count[engine] += 1
        self.items[engine].append((fn, after, self.sems[engine], 1))
        return (self.sems[engine], self.count[engine], engine)

    def bare(self, engine, fn, *after):
        self.items[engine].append((fn, after, None, 0))

    def dma(self, engine, lane, fn, *after):
        lane.count += 16
        self.items[engine].append((fn, after, lane.sem, 16))
        return (lane.sem, lane.count, lane.sem)

    def play(self, engine, eng):
        seen = {}
        for fn, after, sem, n in self.items[engine]:
            for s, value, key in after:
                if seen.get(key, 0) < value:
                    eng.wait_ge(s, value)
                    seen[key] = value
            i = fn(eng)
            if sem:
                i.then_inc(sem, n)


class Lane:

    def __init__(self, sem):
        self.sem, self.count = sem, 0


class Ring:

    def __init__(self, bufs):
        self.bufs, self.free, self.at = bufs, [() for _ in bufs], -1
        self.held = set()

    def take(self):
        assert len(self.held) < len(self.bufs)
        self.at = (self.at + 1) % len(self.bufs)
        while self.at in self.held:
            self.at = (self.at + 1) % len(self.bufs)
        self.held.add(self.at)
        return self.at, self.bufs[self.at], self.free[self.at]

    def give(self, i, *after):
        self.held.discard(i)
        self.free[i] = after


def build(nc, x, W_inT, conv_w, W_xT, W_dtT, b_dt, A_log, D_param, W_CT, W_outT, gate_wT,
          W1, b1, W2, b2, sW1, sb1, sW2, sb2, cst, sel, out):
    f32, bf16, i32, u32 = mybir.dt.float32, mybir.dt.bfloat16, mybir.dt.int32, mybir.dt.uint32
    ALU, ACT, AX = mybir.AluOpType, mybir.ActivationFunctionType, mybir.AxisListType

    x1_d = nc.dram_tensor("x1_d", [T, D], f32, kind="Internal").ap()
    xn_d = nc.dram_tensor("xn_d", [T, D], f32, kind="Internal").ap()
    sh_d = nc.dram_tensor("sh_d", [T, D], f32, kind="Internal").ap()
    z_d = nc.dram_tensor("z_d", [2 * T, D], f32, kind="Internal").ap()

    ctx = ExitStack()
    with ctx:
        def sb(name, shape, dt=f32):
            return ctx.enter_context(nc.sbuf_tensor(name, shape, dt))

        def sem(name):
            return ctx.enter_context(nc.semaphore(name))

        lanes = {}

        def lane(name):
            if name not in lanes:
                lanes[name] = Lane(sem("l_" + name))
            return lanes[name]

        q = Queues(sem)
        op, dma = q.op, q.dma

        C = sb("C", [128, CW])
        SEL = sb("SEL", [96, 16], bf16)
        ident, tri, ones = C[:, CI:CI + 128], C[:, CT:CT + 128], C[:, CO:CO + 128]
        iom8, thr, tidx = C[:, CM8:CM8 + 8], C[:, CTH:CTH + 16], C[:, CTI:CTI + NTILE]
        mhalf, eps, prow = C[:, CMH:CMH + 8], C[:, CEP:CEP + 1], C[:, CP:CP + 1]
        i128, vtok = C[:, CR:CR + 128], C[:, CV:CV + 64]
        wxz = sb("wxz", [128, 2, 512])
        wx = sb("wx", [128, 2, 176])
        wdc = sb("wdc", [80, 256])
        wout = sb("wout", [128, 2, 256])
        wg = sb("wg", [128, 2, 8])
        cw = sb("cw", [128, 2, 3])
        bdt = sb("bdt", [128, 2])
        nea = sb("nea", [128, 2, 16])
        Dp = sb("Dp", [128, 2])
        s1 = sb("s1", [128, 2, F])
        s2 = sb("s2", [128, 8, D])
        sb1t = sb("sb1t", [128, 8])
        sb2t = sb("sb2t", [128, D])
        lg = sb("lg", [128, NTOK, 8])
        wts = sb("wts", [128, 2, NTOK])
        texp = sb("texp", [128, NTILE], i32)
        idg = sb("idg", [128, NCOL], i32)
        ids = sb("ids", [128, NCOL], i32)
        stats2 = [sb(f"stats{i}", [128, 8, 6]) for i in range(2)]
        mv2 = [sb(f"mv{i}", [128, 8, 2]) for i in range(2)]
        rs2 = [sb(f"rs{i}", [128, 8]) for i in range(2)]
        nm2 = [sb(f"nm{i}", [128, 8]) for i in range(2)]
        ARENA = 45060
        arena = sb("arena", [128, ARENA])
        at = [0]

        def cut(n):
            at[0] += n
            assert at[0] <= ARENA, at[0]
            return arena[:, at[0] - n:at[0]]

        PSUM = ctx.enter_context(nc.psum_tensor("psum", [128, 8 * 512], f32))
        PS = [PSUM[:, 512 * i:512 * i + 512] for i in range(8)]

        def load(dst, src, name="w"):
            return dma("sync", lane(name), lambda e: e.dma_start(dst, src))

        def rows8(a):
            return a.rearrange("(j p) d -> p j d", p=128)

        ringN = Ring([cut(2048).rearrange("p (c t) -> p c t", c=2) for _ in range(2)])
        hT = cut(2048).rearrange("p (f t) -> p f t", f=8)
        ringO = Ring([cut(512).rearrange("p (j d) -> p j d", j=2) for _ in range(2)])
        kept = at[0]
        ringX1 = Ring([cut(512).rearrange("p (j d) -> p j d", j=2) for _ in range(2)])
        TA = cut(2052)
        TBb = cut(2048)
        xnb = TA[:, 0:2048].rearrange("p (j d) -> p j d", j=8)
        xcp = TA.rearrange("p (c t) -> p c t", c=2)
        btmp = [TA[0:96, 0:1024], TA[0:96, 1024:2048]]
        xnT = TBb.rearrange("p (c t) -> p c t", c=2)
        spt = xnT
        xs, dts = [[cut(2048).rearrange("p (c t) -> p c t", c=2) for _ in range(2)] for _ in range(2)]
        us = cut(2048).rearrange("p (c t) -> p c t", c=2)
        zsl = [cut(2048).rearrange("p (j d) -> p j d", j=8) for _ in range(2)]
        dcb = [cut(1024) for _ in range(2)]
        bst = [cut(512).bitcast(bf16) for _ in range(2)]
        ringA = Ring([cut(1024) for _ in range(4)])
        ringS = Ring([cut(1024) for _ in range(7)])
        PA, PB = cut(2048), cut(2048)
        yb = PA.rearrange("p (c t) -> p c t", c=2)
        gb = nb = PB.rearrange("p (j d) -> p j d", j=8)

        gen = Ring(PS[4:8])
        bbr = Ring([PSUM[:, 0:1024], PSUM[:, 1024:2048]])

        st = {"ln": 0, ("ln", 0): (), ("ln", 1): (), "TA": (), "TB": (), "PA": (), "PB": (), "hT": (), "u": [(), ()]}
        R = {}
        x_t = {}

        def load_x(b):
            for h in range(4):
                x_t[b, h] = dma("sync", lane(f"x{h}"), lambda e, h=h: e.dma_start(
                    xnb[:, 2 * h:2 * h + 2, :], rows8(x[b])[:, 2 * h:2 * h + 2, :]), *st["TA"])

        load_x(0)
        load(C[:, :], cst)
        load(cw[:, :, :], conv_w.rearrange("(c p) k -> p c k", p=128))
        t_c = load(wxz[:, :, :], W_inT.rearrange("(c p) e -> p c e", p=128))
        z_wx = op("gpsimd", lambda e: e.memset(wx[:, :, :], 0.0))
        wxv = W_xT.rearrange("(c p) e -> p c e", p=128)
        pieces = [(0, 0, 64), (64, 80, 16)] + [(80 + 32 * g, 64, 16) for g in range(3)]
        for to, fr, n in pieces:
            t_wx = dma("sync", lane("wx"), lambda e, to=to, fr=fr, n=n: e.dma_start(
                wx[:, :, to:to + n], wxv[:, :, fr:fr + n]), z_wx)
        load(wdc[0:64, :], W_dtT, "v")
        load(wdc[64:80, :], W_CT, "v")
        load(bdt[:, :], b_dt, "v")
        load(nea[:, :, :], A_log.rearrange("(c p) n -> p c n", p=128), "v")
        load(SEL[:, :], sel, "v")
        load(Dp[:, :], D_param, "v")
        load(wout[:, :, :], W_outT.rearrange("(c p) e -> p c e", p=128), "v")
        t_v = load(wg[:, :, :], gate_wT.rearrange("(c p) e -> p c e", p=128), "v")
        load(s1[:, :, :], sW1.rearrange("(c p) f -> p c f", p=128), "s")
        load(s2[:, :, :], sW2.rearrange("(c p) h -> p c h", p=128), "s")
        load(sb1t[:, :], sb1, "s")
        t_s = load(sb2t[:, :], sb2.unsqueeze(0).to_broadcast([128, D]), "s")
        def exp_ln():
            q.bare("scalar", lambda e: e.preload_act_table_set("natural_log_exp_and_others"))

        exp_ln()
        t_ea = op("scalar", lambda e: e.activation(nea[:, :, :], nea[:, :, :], ACT.Exp), t_v)
        t_nea = op("gpsimd", lambda e: e.tensor_scalar(
            nea[:, :, :], nea[:, :, :], -1.0, None, ALU.mult), t_ea)

        def layernorm(src, dst, w, *ready, free=(), both=False):
            u = st["ln"] = (st["ln"] + 1) % 2
            stats, mv, rs, nm = stats2[u], mv2[u], rs2[u], nm2[u]
            for j in range(8):
                t = op("vector", lambda e, j=j: e.bn_stats(stats[:, j, :], src(j)), *ready[j])
            for j in range(8):
                t = op("vector", lambda e, j=j: e.bn_aggr(mv[:, j, :], stats[:, j, :]), t, *st["ln", u])
            t = op("vector", lambda e: e.tensor_scalar(rs[:, :], mv[:, :, 1], eps, None, ALU.add), t)
            t = op("gpsimd", lambda e: e.tensor_tensor(rs[:, :], rs[:, :], mhalf, ALU.pow), t)
            yield
            t = op("vector", lambda e: e.scalar_tensor_tensor(
                nm[:, :], mv[:, :, 0], -1.0, rs[:, :], ALU.mult, ALU.mult), t)
            for j in range(8):
                if both and j // 2 % 2:
                    w.append(op("vector", lambda e, j=j: e.tensor_scalar(
                        dst(j), src(j), rs[:, j:j + 1], nm[:, j:j + 1], ALU.mult, ALU.add), t, *free))
                    continue
                w.append(op("scalar", lambda e, j=j: e.activation(
                    dst(j), src(j), ACT.Identity, bias=nm[:, j:j + 1], scale=rs[:, j:j + 1]), t, *free))
            st["ln", u] = tuple(w[-4:])
            yield
            yield

        def transposed(src, dst, after, free, w):
            def out(i, ps, h, c, t):
                t = op("scalar", lambda e: e.copy(dst[:, c, 512 * h:512 * h + 512], ps), t, *free)
                gen.give(i, t)
                w[h].append(t)

            held = None
            for h in range(2):
                w.append([])
                for c in range(2):
                    i, ps, fr = gen.take()
                    for j in range(4):
                        t = op("tensor", lambda e, j=j, c=c, h=h, ps=ps: e.transpose(
                            ps[:, 128 * j:128 * j + 128], src(4 * h + j)[:, 128 * c:128 * c + 128],
                            ident), t_c, after[4 * h + j], *fr)
                    if held:
                        out(*held)
                    held = (i, ps, h, c, t)
                    yield
            out(*held)
            yield

        def prep_a(b):
            r = R[b] = {"xt": [], "a": []}
            w, xt, a = [], r["xt"], r["a"]
            yield from layernorm(lambda j: xnb[:, j, :], lambda j: xnb[:, j, :], w,
                                 *[(x_t[b, j // 2], t_c) for j in range(8)], both=b == 0)
            yield from transposed(lambda j: xnb[:, j, :], xnT, w, st["TB"], xt)
            a += [op("gpsimd", lambda e: e.memset(xcp[:, :, 0:1], 0.0), xt[1][1]),
                  op("gpsimd", lambda e: e.memset(xcp[:, :, 1025:1026], 0.0), xt[1][1])]
            for c in range(2):
                for h in range(2):
                    i, ps, fr = gen.take()
                    for k in range(2):
                        t = op("tensor", lambda e, c=c, h=h, k=k, ps=ps: e.matmul(
                            ps, wxz[:, k, 128 * c:128 * c + 128],
                            xnT[:, k, 512 * h:512 * h + 512], start=k == 0, stop=k == 1), *xt[h], *fr)
                    t = op("scalar", lambda e, c=c, h=h, ps=ps: e.copy(
                        xcp[:, c, 1 + 512 * h:513 + 512 * h], ps), t, xt[1][1])
                    gen.give(i, t)
                    a.append(t)
                    yield

        def prep_b(b):
            p, r = b % 2, R[b]
            xt, a = r["xt"], r["a"]
            cv, txs = [], []

            def conv(c):
                t = op("vector", lambda e: e.tensor_scalar(
                    xs[p][:, c, :], xcp[:, c, 1:1025], cw[:, c, 1:2], None, ALU.mult), *a[0:2], *a[2 + 2 * c:4 + 2 * c],
                    *st.get(f"xs{p}", ()))
                t = op("vector", lambda e: e.scalar_tensor_tensor(
                    xs[p][:, c, :], xcp[:, c, 0:1024], cw[:, c, 0:1], xs[p][:, c, :], ALU.mult, ALU.add), t)
                cv.append(op("vector", lambda e: e.scalar_tensor_tensor(
                    xs[p][:, c, :], xcp[:, c, 2:1026], cw[:, c, 2:3], xs[p][:, c, :], ALU.mult, ALU.add), t))

            def gate():
                for g in range(4):
                    i, ps, fr = gen.take()
                    for j in range(2):
                        for k in range(2):
                            t = op("tensor", lambda e, g=g, j=j, k=k, ps=ps: e.matmul(
                                ps[:, 256 * j:256 * j + 256], xnT[:, k, 128 * (2 * g + j):128 * (2 * g + j) + 128],
                                wxz[:, k, 256:512], start=k == 0, stop=k == 1), *xt[1], *fr)
                    z = op("scalar", lambda e, g=g, ps=ps: e.copy(
                        zsl[p][:, 2 * g:2 * g + 2, :], ps), t, *st.get(f"zs{p}", ()))
                    gen.give(i, z)
                    if g % 2 == 0:
                        conv(g // 2)
                    yield
                st["TB"] = (t,)
                r["z"] = z

            yield from gate()
            for c in range(2):
                txs.append(op("scalar", lambda e, c=c: e.activation(
                    xs[p][:, c, :], xs[p][:, c, :], ACT.Silu), cv[c]))
            r["xs"] = txs[1]
            r["zs"] = op("scalar", lambda e: e.activation(zsl[p], zsl[p], ACT.Silu), r["z"])
            exp_ln()
            yield
            yield
            tdc, tb = [], []
            for h in range(2):
                sl = slice(512 * h, 512 * h + 512)
                i, ps, fr = gen.take()
                for k in range(2):
                    t = op("tensor", lambda e, sl=sl, k=k, ps=ps: e.matmul(
                        ps[0:80, :], wx[:, k, 0:80], xs[p][:, k, sl],
                        start=k == 0, stop=k == 1), *txs, t_wx, *fr)
                t = op("scalar", lambda e, sl=sl, ps=ps: e.copy(
                    dcb[p][0:80, sl], ps[0:80, :]), t, *st.get(f"dc{p}", ()))
                tdc.append(t)
                gen.give(i, t)
                yield
            r["dc"] = tdc[1]
            for h in range(2):
                sl = slice(512 * h, 512 * h + 512)
                i, ps, fr = gen.take()
                for k in range(2):
                    tm = op("tensor", lambda e, sl=sl, k=k, ps=ps: e.matmul(
                        ps[0:96, :], wx[:, k, 80:176], xs[p][:, k, sl],
                        start=k == 0, stop=k == 1), *fr)
                tm = op("scalar", lambda e, sl=sl, ps=ps: e.copy(btmp[0][:, sl], ps[0:96, :]), tm, *cv)
                gen.give(i, tm)
                tb.append(tm)
                yield
            t = op("vector", lambda e: e.tensor_copy(bst[p][0:96, :], btmp[0]), *tb, *st.get(f"bst{p}", ()))
            t = op("vector", lambda e: e.tensor_tensor(btmp[1], btmp[0], bst[p][0:96, :], ALU.subtract), t)
            t1 = op("vector", lambda e: e.tensor_copy(bst[p][0:64, :], btmp[1][0:64, :]), t)
            t = op("vector", lambda e: e.tensor_tensor(
                btmp[0][0:32, :], btmp[1][0:32, :], bst[p][0:32, :], ALU.subtract), t1)
            r["bst"] = op("vector", lambda e: e.tensor_copy(bst[p][0:32, :], btmp[0][0:32, :]), t)
            st["TA"] = (r["bst"],)
            if b + 1 < NB:
                load_x(b + 1)
            yield
            v, m = [], []
            for h in range(2):
                sl = slice(512 * h, 512 * h + 512)
                for c in range(2):
                    i, ps, fr = gen.take()
                    t = op("tensor", lambda e, c=c, sl=sl, ps=ps: e.matmul(
                        ps, wdc[0:64, 128 * c:128 * c + 128], dcb[p][0:64, sl],
                        start=True, stop=True), tdc[h], t_v, *fr)
                    u = op("scalar", lambda e, c=c, sl=sl, ps=ps: e.activation(
                        dts[p][:, c, sl], ps, ACT.Relu, bias=bdt[:, c:c + 1]),
                        t, *st.get(f"dt{p}", ()))
                    t = op("scalar", lambda e, c=c, sl=sl, ps=ps: e.activation(
                        spt[:, c, sl], ps, ACT.Abs, bias=bdt[:, c:c + 1]), t, *st["TB"])
                    gen.give(i, u, t)
                    v.append(t)
                    m.append(u)
                yield
            t = op("scalar", lambda e: e.activation(spt, spt, ACT.Exp, scale=-1.0), *v)
            t = op("scalar", lambda e: e.activation(spt, spt, ACT.Ln, bias=1.0), t)
            yield
            r["dt"] = op("vector", lambda e: e.scalar_tensor_tensor(
                dts[p], spt, 1e-5, dts[p], ALU.add, ALU.add), t, *m)
            st["TB"] = (r["dt"],)
            yield

        def scaled(b, c, engine):
            r, p = R[b], b % 2
            r["u", c] = op(engine, lambda e: e.tensor_tensor(
                us[:, c, :], dts[p][:, c, :], xs[p][:, c, :], ALU.mult), r["dt"], r["xs"], *st["u"][c])

        Y = []

        def yout():
            if not Y:
                return
            b, c, i_s, S0, t_sum = Y.pop()
            p, r = b % 2, R[b]
            for h in range(2):
                sl = slice(512 * h, 512 * h + 512)
                i, ps, fr = gen.take()
                tc = op("tensor", lambda e, sl=sl, ps=ps: e.matmul(
                    ps, wdc[64:80, 128 * c:128 * c + 128], dcb[p][64:80, sl],
                    start=True, stop=True), r["dc"], *fr)
                yield
                t = op("vector", lambda e, sl=sl, ps=ps: e.tensor_tensor(
                    yb[:, c, sl], S0[:, sl], ps, ALU.mult), t_sum, tc, *st["PA"])
                gen.give(i, t)
            ringS.give(i_s, t)
            st[f"dc{p}"] = (tc,)
            t = op("vector", lambda e: e.scalar_tensor_tensor(
                yb[:, c, :], xs[p][:, c, :], Dp[:, c:c + 1], yb[:, c, :], ALU.mult, ALU.add), t, r["xs"])
            if c == 1:
                r["y"] = t
                st[f"xs{p}"] = (t, r["u", 0], r["u", 1])

        AHEAD, YOUT = 3, 2

        def main(b):
            p, r = b % 2, R[b]
            bb_of, a_of = {}, {}

            def spread(k):
                i, bb, fr = bbr.take()
                n = k % 16
                for h in range(2):
                    t = op("tensor", lambda e, h=h: e.matmul(
                        bb[:, 512 * h:512 * h + 512], SEL[:, n:n + 1].to_broadcast([96, 128]),
                        bst[p][0:96, 512 * h:512 * h + 512], start=True, stop=True), r["bst"], t_v, *fr)
                bb_of[k] = (i, bb, t)
                st[f"bst{p}"] = (t,)

            def decay(k):
                i, A, fr = ringA.take()
                c, n = k // 16, k % 16
                t = op("scalar", lambda e: e.activation(
                    A, dts[p][:, c, :], ACT.Exp, scale=nea[:, c, n:n + 1]), r["dt"], t_nea, *fr)
                a_of[k] = (i, A, t)
                st[f"dt{p}"] = (t, r["u", 0], r["u", 1]) if k == 31 else ()

            spread(0)
            for k in range(AHEAD):
                decay(k)
            for k in range(32):
                c, n = k // 16, k % 16
                if k == 6:
                    scaled(b, 1, "gpsimd")
                if k + AHEAD < 32:
                    decay(k + AHEAD)
                if k < 31:
                    spread(k + 1)
                i, bb, t_b = bb_of[k]
                t = op("vector", lambda e, bb=bb, c=c: e.tensor_tensor(
                    bb, us[:, c, :], bb, ALU.mult), t_b, r["u", c])
                st["u"][c] = (t,)
                i_s, S, fs = ringS.take()
                ia, A, t_a = a_of[k]
                t_sc = op("vector", lambda e, A=A, bb=bb, S=S: e.tensor_tensor_scan(
                    S, A, bb, 0.0, ALU.mult, ALU.add), t_a, t, *fs)
                ringA.give(ia, t_sc)
                bbr.give(i, t_sc)
                if n == 0:
                    S0, i0, t_p = S, i_s, t_sc
                else:
                    t_p = op("gpsimd", lambda e, S=S, S0=S0: e.tensor_tensor(S0, S0, S, ALU.add), t_p, t_sc)
                    ringS.give(i_s, t_p)
                if n == 15:
                    Y.append((b, c, i0, S0, t_p))
                if n == YOUT:
                    ending = yout()
                if n >= YOUT:
                    next(ending, None)
                yield

        def post(b):
            p, r = b % 2, R[b]
            gt = []

            def gated(g, i, ps, t):
                t = op("vector", lambda e: e.tensor_tensor(
                    gb[:, 2 * g:2 * g + 2, :], zsl[p][:, 2 * g:2 * g + 2, :],
                    ps.rearrange("p (j d) -> p j d", j=2), ALU.mult), t, r["zs"], *st["PB"])
                gen.give(i, t)
                gt.extend([t, t])

            held = None
            for g in range(4):
                i, ps, fr = gen.take()
                for j in range(2):
                    for k in range(2):
                        t = op("tensor", lambda e, g=g, j=j, k=k, ps=ps: e.matmul(
                            ps[:, 256 * j:256 * j + 256], yb[:, k, 128 * (2 * g + j):128 * (2 * g + j) + 128],
                            wout[:, k, :], start=k == 0, stop=k == 1), r["y"], *fr)
                st["PA"] = (t,)
                if held:
                    gated(*held)
                held = (g, i, ps, t)
                yield
            gated(*held)
            st[f"zs{p}"] = r["gated"] = (gt[-1],)
            w = []
            yield from layernorm(lambda j: gb[:, j, :], lambda j: gb[:, j, :], w, *[(t,) for t in gt],
                                 both=b == NB - 1)
            ta = []
            for h in range(4):
                sl = slice(2 * h, 2 * h + 2)
                ix, X1, fx = ringX1.take()
                t_x = dma("sync", lane(f"X{ix}"), lambda e, X1=X1, sl=sl: e.dma_start(
                    X1, rows8(x[b])[:, sl, :]), *fx)
                ta.append(op("vector" if b == NB - 1 else "gpsimd", lambda e, sl=sl, X1=X1: e.tensor_tensor(
                    gb[:, sl, :], X1, gb[:, sl, :], ALU.add), *w[2 * h:2 * h + 2], t_x))
                ringX1.give(ix, ta[-1])
            o1 = dma("sync", lane("x1"), lambda e: e.dma_start(
                rows8(x1_d[TB * b:TB * (b + 1), :]), gb), ta[3])
            yield
            w = []
            yield from layernorm(lambda j: gb[:, j, :], lambda j: nb[:, j, :], w,
                                 *[(ta[j // 2],) for j in range(8)], free=(o1,),
                                 both=b == NB - 1)
            o2 = dma("sync", lane("xn"), lambda e: e.dma_start(
                rows8(xn_d[TB * b:TB * (b + 1), :]), nb), *w[4:8])
            r["stored"] = (o1, o2)
            xt = []
            i_n, nT, fn = ringN.take()
            yield from transposed(lambda j: nb[:, j, :], nT, w, fn, xt)
            r["nT"] = (i_n, nT, xt)
            st["PB"] = (o2, xt[1][1])
            i, ps, fr = gen.take()
            for j in range(8):
                for k in range(2):
                    t = op("tensor", lambda e, j=j, k=k, ps=ps: e.matmul(
                        ps[:, 8 * j:8 * j + 8], nT[:, k, 128 * j:128 * j + 128], wg[:, k, :],
                        start=k == 0, stop=k == 1), *xt[j // 4], *fr)
            t = op("scalar", lambda e, ps=ps: e.copy(
                lg[:, 8 * b:8 * b + 8, :], ps[:, 0:64].rearrange("p (j e) -> p j e", j=8)), t)
            gen.give(i, t)
            r["lg"] = t
            yield

        def shared(b):
            r = R[b]
            i_n, nT, nts = r["nT"]
            for g in range(4):
                xt, direct = nts[g // 2], "direct" in st
                fn = ACT.Gelu if direct else ACT.Identity
                hw = []

                def out(f, i, ps, t, fn=fn):
                    for a in range(2):
                        t = op("scalar", lambda e, a=a: e.activation(
                            hT[:, f + a, :], ps[:, 256 * a:256 * a + 256], fn,
                            bias=sb1t[:, f + a:f + a + 1]), t, *st["hT"])
                        hw.append(t)
                    gen.give(i, t)

                held = None
                for f in range(0, 8, 2):
                    i, ps, fr = gen.take()
                    for a in range(2):
                        for k in range(2):
                            t = op("tensor", lambda e, f=f + a, a=a, k=k, g=g, ps=ps: e.matmul(
                                ps[:, 256 * a:256 * a + 256], s1[:, k, 128 * f:128 * f + 128],
                                nT[:, k, 256 * g:256 * g + 256], start=k == 0, stop=k == 1), t_s, *xt, *fr)
                    if g == 3 and f == 6:
                        ringN.give(i_n, t, r["lg"])
                    if held:
                        out(*held)
                    held = (f, i, ps, t)
                    yield
                out(*held)
                if not direct:
                    hw = [op("scalar", lambda e: e.activation(hT, hT, ACT.Gelu), hw[7])] * 8
                    exp_ln()
                    yield True
                    yield True
                    yield True
                i, ps, fr = gen.take()
                for j in range(2):
                    for f in range(8):
                        t = op("tensor", lambda e, j=j, f=f, ps=ps: e.matmul(
                            ps[:, 256 * j:256 * j + 256], hT[:, f, 128 * j:128 * j + 128], s2[:, f, :],
                            start=f == 0, stop=f == 7), hw[f], *fr)
                        if f % 4 == 3:
                            yield
                st["hT"] = (t,)
                yield True
                io, O, fo = ringO.take()
                for j in range(2):
                    t2 = op("vector", lambda e, j=j, ps=ps, O=O: e.tensor_tensor(
                        O[:, j, :], sb2t[:, :], ps[:, 256 * j:256 * j + 256], ALU.add), t, t_s, *fo)
                gen.give(i, t2)
                o = dma("sync", lane(f"sh{io}"), lambda e, g=g, O=O: e.dma_start(
                    rows8(sh_d[TB * b + 256 * g:TB * b + 256 * g + 256, :]), O), t2)
                ringO.give(io, o)
                r.setdefault("sh", []).append(o)

        def chain(*gens):
            for g in gens:
                yield from g

        def part(side, n):
            for _ in range(n):
                if next(side, None):
                    break

        def experts():
            for b in range(NB - 1):
                while "lg" not in R.get(b, ()):
                    yield
                yield from shared(b)

        beside = experts()
        POST, PREP, NPOST, NPREP = 5, 9, 18, 17
        QUOTA, LEAST = [0, 2, 3, 2], [0, 1, 1, 2]
        for _ in chain(prep_a(0), prep_b(0)):
            pass
        scaled(0, 0, "vector")
        for b in range(NB):
            ahead = prep_a(b + 1) if b + 1 < NB else iter(())
            late = prep_b(b + 1) if b + 1 < NB else iter(())
            behind = post(b - 1) if b else iter(())
            n_post = n_prep = 0
            for k, _ in enumerate(main(b)):
                n_was = n_post + n_prep - (k < PREP)
                if k >= POST:
                    want = -(-NPOST * (k + 1 - POST) // (31 - POST))
                    part(behind, want - n_post)
                    n_post = want
                if k < PREP:
                    part(ahead, 1)
                else:
                    part(ahead, 99)
                    while b and "gated" not in R[b - 1]:
                        part(behind, 1)
                    want = -(-NPREP * (k + 1 - PREP) // (31 - PREP))
                    part(late, want - n_prep)
                    n_prep = want
                part(beside, max(LEAST[b], QUOTA[b] - (n_post + n_prep - n_was)))
            part(behind, 99)
            part(late, 99)
            if b + 1 < NB:
                scaled(b + 1, 0, "vector")
        for _ in yout():
            pass
        for _ in post(NB - 1):
            part(beside, 3)
        st["direct"] = True
        last = [(q.sems[e], q.count[e], e) for e in q.ENGINES if q.count[e]]
        for b in range(NB):
            last += list(R[b]["stored"])

        fill = chain(beside, shared(NB - 1))

        def filler(n):
            for _ in range(n):
                next(fill, None)

        at[0] = kept
        oh_at = at[0]
        OHp = cut(2 * 4096).rearrange("p (n m) -> p n m", m=128)
        OHq = cut(2 * 32 * NCOL).rearrange("p (n m) -> p n m", m=NCOL)
        rb = cut(256 * 12)
        at3 = [0]

        def r3(n=256):
            at3[0] += n
            return rb[:, at3[0] - n:at3[0]]

        def v3(a):
            return a.rearrange("p (j e) -> p j e", e=8)

        def over_e(a):
            return a.unsqueeze(2).to_broadcast([128, NTOK, 8])

        def over_j(a):
            return a.unsqueeze(1).to_broadcast([128, NTOK, 8])

        pr, oh1, oh2, eq, M, pre, tot, inc = (r3() for _ in range(8))
        mx, z, ix, m1, m2, cnt = (r3(32) for _ in range(6))
        nt, ts, te, bs = (r3(8) for _ in range(4))
        ntb = r3(128)
        te8 = cut(NTILE * 8)
        texf = cut(NTILE)
        posi, qi, pi = (cut(64).bitcast(i32) for _ in range(3))
        posf, qf, pf = cut(64), cut(64), cut(64)
        vt, ve, vi = cut(NCOL), cut(NCOL), cut(NCOL).bitcast(i32)

        def dve(fn, *after):
            return op("vector", fn, *after)

        t = dve(lambda e: e.reduce_max(mx, lg[:, :, :], axis=AX.X), *last)
        t = dve(lambda e: e.tensor_tensor(v3(pr), lg[:, :, :], over_e(mx), ALU.subtract), t)
        t = op("scalar", lambda e: e.activation(pr, pr, ACT.Exp), t)
        t = dve(lambda e: e.reduce_sum(z, v3(pr), axis=AX.X), t)
        t = dve(lambda e: e.reciprocal(z, z), t)
        t = dve(lambda e: e.tensor_tensor(v3(pr), v3(pr), over_e(z), ALU.mult), t)

        def best(oh, m, t):
            t = dve(lambda e: e.reduce_max(m, v3(pr), axis=AX.X), t)
            t = dve(lambda e: e.tensor_tensor(v3(eq), v3(pr), over_e(m), ALU.is_equal), t)
            t = dve(lambda e: e.tensor_tensor(v3(eq), v3(eq), over_j(iom8), ALU.mult), t)
            t = dve(lambda e: e.tensor_reduce(ix, v3(eq), axis=AX.X, op=ALU.min), t)
            return dve(lambda e: e.tensor_tensor(v3(oh), over_e(ix), over_j(iom8), ALU.is_equal), t)

        t = best(oh1, m1, t)
        t = dve(lambda e: e.scalar_tensor_tensor(pr, oh1, -2.0, pr, ALU.mult, ALU.add), t)
        t = best(oh2, m2, t)
        t_m = dve(lambda e: e.tensor_tensor(M, oh1, oh2, ALU.add), t)
        FILL = 6
        filler(8)
        op("tensor", lambda e: e.matmul(PS[0][:, 0:256], tri, M, start=True, stop=True), t_m, *last)
        t = op("tensor", lambda e: e.matmul(PS[1][:, 0:256], ones, M, start=True, stop=True), t_m)
        t = dve(lambda e: e.tensor_copy(tot, PS[1][:, 0:256]), t)
        dve(lambda e: e.tensor_copy(pre, PS[0][:, 0:256]))
        for x8 in range(8):
            t2 = dve(lambda e, x8=x8: e.tensor_tensor_scan(
                v3(inc)[:, :, x8], ones[:, 0:NTOK], v3(tot)[:, :, x8], 0.0, ALU.mult, ALU.add), t)
        t = dve(lambda e: e.tensor_copy(cnt[:, 0:8], v3(inc)[:, NTOK - 1, :]), t2)
        nt3 = ntb.rearrange("p (e i) -> p e i", i=16)
        t = dve(lambda e: e.tensor_tensor(nt3, cnt[:, 0:8].unsqueeze(2).to_broadcast([128, 8, 16]),
                                          thr.unsqueeze(1).to_broadcast([128, 8, 16]), ALU.is_gt), t)
        t = dve(lambda e: e.reduce_sum(nt, nt3, axis=AX.X), t)
        t_te = dve(lambda e: e.tensor_tensor_scan(te, ones[:, 0:8], nt, 0.0, ALU.mult, ALU.add), t)
        te3 = te8.rearrange("p (i e) -> p i e", e=8)
        t8 = dve(lambda e: e.tensor_tensor(te3, tidx.unsqueeze(2).to_broadcast([128, NTILE, 8]),
                                           te.unsqueeze(1).to_broadcast([128, NTILE, 8]), ALU.is_ge), t_te)
        t = dve(lambda e: e.tensor_tensor(ts, te, nt, ALU.subtract), t_te)
        t8 = dve(lambda e: e.reduce_sum(texf, te3, axis=AX.X), t8)
        t = dve(lambda e: e.tensor_scalar(bs, ts, float(ROWS), None, ALU.mult), t)
        t_ex = dve(lambda e: e.tensor_scalar(texp[:, :], texf, 7.0, None, ALU.min), t8)
        t2 = dve(lambda e: e.tensor_tensor(pre, pre, inc, ALU.add), t2)
        t2 = dve(lambda e: e.tensor_tensor(pre, pre, tot, ALU.subtract), t2)
        t = dve(lambda e: e.tensor_tensor(v3(pre), v3(pre), over_j(bs), ALU.add), t, t2)
        for k, oh in enumerate((oh1, oh2)):
            t1 = dve(lambda e, oh=oh: e.tensor_tensor(oh, oh, pre, ALU.mult), t)
            t1 = dve(lambda e, k=k, oh=oh: e.reduce_sum(posf[:, 32 * k:32 * k + 32], v3(oh), axis=AX.X), t1)
        t = dve(lambda e: e.tensor_copy(posi, posf), t1)
        tq = dve(lambda e: e.tensor_scalar(qi, posi, 7, None, ALU.logical_shift_right), t)
        tp = dve(lambda e: e.tensor_scalar(pi, posi, 127, None, ALU.bitwise_and), t)
        tq = dve(lambda e: e.tensor_copy(qf, qi), tq)
        tp = dve(lambda e: e.tensor_copy(pf, pi), tp)
        TAB = PS[2][:, 0:NCOL]
        for h in range(4):
            sl = slice(16 * h, 16 * h + 16)
            t = dve(lambda e, sl=sl: e.tensor_tensor(
                OHq[:, sl, :], qf[:, sl].unsqueeze(2).to_broadcast([128, 16, NCOL]),
                i128[:, 0:NCOL].unsqueeze(1).to_broadcast([128, 16, NCOL]), ALU.is_equal), tq)
            t1 = dve(lambda e, sl=sl: e.tensor_tensor(
                OHp[:, sl, :], pf[:, sl].unsqueeze(2).to_broadcast([128, 16, 128]),
                i128.unsqueeze(1).to_broadcast([128, 16, 128]), ALU.is_equal), tp)
            t = dve(lambda e, sl=sl: e.tensor_tensor(
                OHq[:, sl, :], OHq[:, sl, :], vtok[:, sl].unsqueeze(2).to_broadcast([128, 16, NCOL]), ALU.mult), t)
            filler(FILL)
            for n in range(16 * h, 16 * h + 16):
                t2 = op("tensor", lambda e, n=n: e.matmul(
                    TAB, OHp[:, n, :], OHq[:, n, :], start=n == 0, stop=n == 63), t, t1)
        t = dve(lambda e: e.tensor_scalar(vt, TAB, float(2 * T), None, ALU.add), t2)
        t_v2 = dve(lambda e: e.tensor_copy(ids[:, :], vt), t)
        t_idg = dve(lambda e: e.tensor_scalar(idg[:, :], ids[:, :], T - 1, None, ALU.bitwise_and), t_v2)
        t = dve(lambda e: e.tensor_tensor(z, m1, m2, ALU.add))
        t = dve(lambda e: e.reciprocal(z, z), t)
        dve(lambda e: e.tensor_tensor(wts[:, 0, :], m1, z, ALU.mult), t)
        t_w = dve(lambda e: e.tensor_tensor(wts[:, 1, :], m2, z, ALU.mult), t)

        routing_end = at[0]

        w1v = W1.rearrange("e (c p) f -> e p c f", p=128)
        w2v = W2.rearrange("e (c p) h -> e p c h", p=128)
        NW = 2
        ringW = Ring([(cut(2048).rearrange("p (c f) -> p c f", c=2),
                       cut(2048).rearrange("p (c h) -> p c h", c=8), cut(8), cut(256)) for _ in range(NW)])
        ringG = Ring([cut(512).rearrange("p (j d) -> p j d", j=2) for _ in range(3)])
        ringX = Ring([cut(512).rearrange("p (c t) -> p c t", c=2) for _ in range(2)])
        ringH = Ring([cut(2048).rearrange("p (f t) -> p f t", f=8) for _ in range(2)])
        ringY = Ring([cut(512).rearrange("p (j d) -> p j d", j=2) for _ in range(3)])
        pX, pH, pY = Ring(PS[0:2]), Ring(PS[3:6]), Ring(PS[6:8])
        table = [(q.sems["vector"], q.count["vector"], "vector")]
        regs = {}

        def read(i):
            def fn(e):
                regs[i] = e.value_load(texp[0:1, i:i + 1], min_val=0, max_val=E - 1)
                return e.dma_start(Ws[i][1][0], w1v[bass.ds(regs[i], 1)].squeeze(0))
            return fn

        def piece(i, n, src):
            return lambda e: e.dma_start(Ws[i][1][n], src(regs[i]))

        Ws, G, XT = {}, {}, {}

        def weights(i):
            iw, W, fw = ringW.take()
            Ws[i] = (iw, W)
            ln = lane(f"W{iw}")
            dma("sync", ln, read(i), t_ex, *fw, *table, *last)
            dma("sync", ln, piece(i, 1, lambda v: w2v[bass.ds(v, 1)].squeeze(0)))
            dma("sync", ln, piece(i, 2, lambda v: b1[bass.ds(v, 1)].squeeze(0)))
            Ws[i] += (dma("sync", ln, piece(i, 3, lambda v: b2[bass.ds(v, 1)].to_broadcast([128, D]))),)

        def gather(i):
            ig, g, fg = ringG.take()
            for j in range(2):
                t = dma("gpsimd", lane(f"G{ig}"), lambda e, g=g, j=j: e.indirect_dma_start(
                    g[:, j, :], None, xn_d,
                    bass.IndirectOffsetOnAxis(ap=idg[:, 2 * i + j:2 * i + j + 1].bitcast(u32), axis=0)),
                    t_idg, *fg, *table, *last)
            G[i] = (ig, g, t)

        def turn(i):
            ig, g, t_g = G[i]
            ix_, ps, fr = pX.take()
            for c in range(2):
                for j in range(2):
                    t = op("tensor", lambda e, c=c, j=j, ps=ps, g=g: e.transpose(
                        ps[:, 256 * c + 128 * j:256 * c + 128 * j + 128], g[:, j, 128 * c:128 * c + 128],
                        ident), t_g, *done, *fr)
            ringG.give(ig, t)
            ixs, xT, fx = ringX.take()
            t_x = op("vector", lambda e, ps=ps, xT=xT: e.tensor_copy(
                xT, ps.rearrange("p (c t) -> p c t", c=2)), t, *fx)
            pX.give(ix_, t_x)
            XT[i] = (ixs, xT, t_x)

        top, at[0] = at[0], oh_at
        ringL = Ring([tuple(cut(2048).rearrange("p (j d) -> p j d", j=8) for _ in range(2)) for _ in range(NB)])
        assert at[0] <= routing_end
        at[0] = top
        Lb = {}
        for b in range(NB):
            Lb[b] = ringL.take()

        def load_l(b):
            il, (XX, S), fl = Lb[b]
            rows = slice(TB * b, TB * (b + 1))
            dma("sync", lane(f"L{il}"), lambda e, rows=rows, S=S: e.dma_start(
                S, rows8(sh_d[rows, :])), *done, *R[b]["sh"], *fl)
            Lb[b] += (dma("sync", lane(f"L{il}"), lambda e, rows=rows, XX=XX: e.dma_start(
                XX, rows8(x1_d[rows, :])), *R[b]["stored"], *fl),)

        top, at[0] = at[0], 0
        DG = [cut(128) for _ in range(kept // 128)]
        at[0] = top
        DG += [cut(128) for _ in range(2 * NTOK - len(DG))]
        t_dg = {}

        def diagonal(m):
            k, n = m % 2, m // 2
            t_dg[m] = op("vector", lambda e: e.tensor_scalar(
                DG[m], ident, wts[:, k, n:n + 1], None, ALU.mult), t_w, *done, *last,
                *[t for b in range(NB) for t in R[b]["sh"]])

        for i in range(min(NW, NTILE)):
            weights(i)
        for i in range(3):
            gather(i)
        for _ in fill:
            pass
        done = [(q.sems[e], q.count[e], e) for e in ("tensor", "scalar", "vector")]
        turn(0)
        scat = []
        for i in range(NTILE):
            iw, (w1, w2, bb1, bb2), t_wt = Ws[i]
            ixs, xT, t_x = XT[i]
            ih, h, fh = ringH.take()
            hw = []
            for f in range(0, 8, 2):
                ip, ps, fr = pH.take()
                for a in range(2):
                    for k in range(2):
                        t = op("tensor", lambda e, f=f + a, a=a, k=k, ps=ps, w1=w1, xT=xT: e.matmul(
                            ps[:, 256 * a:256 * a + 256], w1[:, k, 128 * f:128 * f + 128], xT[:, k, :],
                            start=k == 0, stop=k == 1), t_x, t_wt, *fr)
                for a in range(2):
                    t2 = op("scalar", lambda e, f=f + a, a=a, ps=ps, h=h, bb1=bb1: e.activation(
                        h[:, f, :], ps[:, 256 * a:256 * a + 256], ACT.Gelu, bias=bb1[:, f:f + 1]), t, t_wt, *fh)
                    hw.append(t2)
                pH.give(ip, t2)
            ringX.give(ixs, t)
            if i + 1 < NTILE:
                turn(i + 1)
            ip, ps, fr = pY.take()
            for j in range(2):
                for f in range(8):
                    t = op("tensor", lambda e, j=j, f=f, ps=ps, h=h, w2=w2: e.matmul(
                        ps[:, 256 * j:256 * j + 256], h[:, f, 128 * j:128 * j + 128], w2[:, f, :],
                        start=f == 0, stop=f == 7), hw[f], *fr)
            ringH.give(ih, t)
            iy, y, fy = ringY.take()
            for j in range(2):
                t2 = op("vector", lambda e, j=j, ps=ps, y=y, bb2=bb2: e.tensor_tensor(
                    y[:, j, :], bb2, ps[:, 256 * j:256 * j + 256], ALU.add), t, t_wt, *fy)
            pY.give(ip, t2)
            ringW.give(iw, t2, t)
            for m in range(2 * i, min(2 * i + 2, 2 * NTOK)):
                diagonal(m)
            if i % 4 == 0 and 2 <= i // 4 < 2 + NB:
                load_l(i // 4 - 2)
            if i + 3 < NTILE:
                gather(i + 3)
            for j in range(2):
                o = dma("gpsimd", lane(f"Y{iy}"), lambda e, i=i, j=j, y=y: e.indirect_dma_start(
                    z_d, bass.IndirectOffsetOnAxis(ap=ids[:, 2 * i + j:2 * i + j + 1].bitcast(u32), axis=0),
                    y[:, j, :], None, bounds_check=2 * T - 1, oob_is_err=False), t2, t_v2)
            ringY.give(iy, o)
            scat = (scat + [o])[-3:]
            if i + NW < NTILE:
                weights(i + NW)

        at[0] = routing_end
        Zs = [tuple(cut(512).rearrange("p (j d) -> p j d", j=2) for _ in range(2)) for _ in range(4 * NB)]
        routed = [(q.sems[e], q.count[e], e) for e in ("tensor", "scalar", "vector")]
        t_zs = []
        for n, Z in enumerate(Zs):
            for k in range(2):
                r0 = T * k + 256 * n
                t_z = dma("sync", lane(f"Z{n}"), lambda e, k=k, Z=Z, r0=r0: e.dma_start(
                    Z[k], rows8(z_d[r0:r0 + 256, :])), *scat, *last, *routed)
            t_zs.append(t_z)

        def normed(b, norm, w, banks):
            for _ in norm:
                pass
            for g in range(4):
                ringB.give(banks[g][0], *w[2 * g:2 * g + 2])

        def finish(b, norm, w, banks):
            il, (XX, S), fl, t_l = Lb[b]
            outs = []
            for h in range(4):
                sl = slice(2 * h, 2 * h + 2)
                t = dve(lambda e, sl=sl: e.tensor_tensor(
                    XX[:, sl, :], XX[:, sl, :], S[:, sl, :], ALU.add), *w[2 * h:2 * h + 2], t_l)
                outs.append(dma("sync", lane(f"out{h}"), lambda e, sl=sl: e.dma_start(
                    rows8(out[b])[:, sl, :], XX[:, sl, :]), t))
            ringL.give(il, *outs)

        ringB = Ring(PS)
        base = {}

        def shared_part(b, g):
            il, (XX, S), fl, t_l = Lb[b]
            ib, ps, fr = ringB.take()
            op("tensor", lambda e: e.matmul(ps, ident, S[:, 2 * g:2 * g + 2, :],
                                            start=True, stop=False), t_l, *fr, *routed)
            base[b, g] = (ib, ps)

        for b in range(2):
            for g in range(4):
                shared_part(b, g)
        held = None
        for b in range(NB):
            il, (XX, S), fl, t_l = Lb[b]
            sw, banks = [], []
            for g in range(4):
                Z, t_z = Zs[4 * b + g], t_zs[4 * b + g]
                if b >= 2:
                    shared_part(b, g)
                ib, ps = base[b, g]
                banks.append((ib, ps))
                for j in range(2):
                    m = 2 * (8 * b + 2 * g + j)
                    o = ps[:, 256 * j:256 * j + 256]
                    op("tensor", lambda e, o=o, j=j, m=m, Z=Z: e.matmul(
                        o, DG[m], Z[0][:, j, :], start=False, stop=False), t_z, t_dg[m])
                    t = op("tensor", lambda e, o=o, j=j, m=m, Z=Z: e.matmul(
                        o, DG[m + 1], Z[1][:, j, :], start=False, stop=j == 1), t_z, t_dg[m + 1])
                sw += [(t,), (t,)]
            w = []
            norm = layernorm(lambda j, B=banks: B[j // 2][1][:, 256 * (j % 2):256 * (j % 2) + 256], lambda j, S=S: S[:, j, :], w, *sw, both=b == NB - 1)
            if held:
                normed(*held)
            next(norm)
            if held:
                finish(*held)
            held = (b, norm, w, banks)
        normed(*held)
        finish(*held)

        block = ctx.enter_context(nc.Block())

        @block.tensor
        def _(eng):
            q.play("tensor", eng)

        @block.vector
        def _(eng):
            q.play("vector", eng)

        @block.scalar
        def _(eng):
            q.play("scalar", eng)

        @block.gpsimd
        def _(eng):
            q.play("gpsimd", eng)

        @block.sync
        def _(eng):
            q.play("sync", eng)
            for ln in lanes.values():
                eng.wait_ge(ln.sem, ln.count)


def kernel(**inputs):
    import numpy as np
    import concourse.bacc as bacc
    from concourse import mybir as mb
    from concourse.bass_utils import run_bass_kernel_spmd as run
    import ml_dtypes

    def a(name):
        return np.ascontiguousarray(inputs[name])

    def t(name):
        return np.ascontiguousarray(np.asarray(inputs[name]).T)

    def cols(name):
        return np.ascontiguousarray(np.asarray(inputs[name]).reshape(-1, 128).T)

    cst = np.zeros((128, CW), np.float32)
    cst[:, CI:CI + 128] = np.eye(128)
    cst[:, CT:CT + 128] = np.triu(np.ones((128, 128)), 1)
    cst[:, CO:CO + 128] = 1.0
    cst[:, CM8:CM8 + 8] = np.arange(8) - 8.0
    cst[:, CTH:CTH + 16] = np.arange(16) * float(ROWS)
    cst[:, CTI:CTI + NTILE] = np.arange(NTILE)
    cst[:, CMH:CMH + 8] = -0.5
    cst[:, CEP] = 1e-5
    cst[:, CP] = np.arange(128)
    cst[:, CR:CR + 128] = np.arange(128)
    cst[:, CV:CV + 64] = np.arange(64) * 128.0 + np.arange(128)[:, None] - 2.0 * T
    sel = np.zeros((96, 16), ml_dtypes.bfloat16)
    for g in range(3):
        sel[32 * g:32 * g + 16] = np.eye(16)
    A, Fp = "L0_attn_", "L0_ffn_"
    arrays = {
        "x": a(A + "x"), "W_inT": t(A + "W_in"), "conv_w": a(A + "conv_w"), "W_xT": t(A + "W_x"),
        "W_dtT": t(A + "W_dt"), "b_dt": cols("L0_attn_b_dt"), "A_log": a(A + "A_log"), "D_param": cols("L0_attn_D_param"),
        "W_CT": t(A + "W_C"), "W_outT": t(A + "W_out"), "gate_wT": t(Fp + "gate_w"),
        "W1": a(Fp + "W1"),
        "b1": np.ascontiguousarray(np.asarray(inputs[Fp + "b1"]).reshape(E, 8, 128).transpose(0, 2, 1)),
        "W2": a(Fp + "W2"), "b2": a(Fp + "b2"), "sW1": a(Fp + "sW1"),
        "sb1": cols("L0_ffn_sb1"),
        "sW2": a(Fp + "sW2"), "sb2": a(Fp + "sb2"),
        "cst": cst, "sel": sel,
    }
    nc = bacc.Bacc("TRN2", target_bir_lowering=False, num_devices=1)
    aps = {n: nc.dram_tensor(n, v.shape, mb.dt.from_np(v.dtype), kind="ExternalInput").ap()
           for n, v in arrays.items()}
    out = nc.dram_tensor("out", (NB, TB, D), mb.dt.float32, kind="ExternalOutput").ap()
    build(nc, out=out, **aps)
    r = run(nc, [arrays], core_ids=[0])
    return r.results[0]["out"]
```
